# Optimizing a Trainium2 kernel written in Bass

```python
import numpy as np
import jax
import jax.numpy as jnp

def _softmax(x, axis=-1):
    return jax.nn.softmax(x, axis=axis)

def _gelu(x):
    return jax.nn.gelu(x, approximate=True)

def _silu(x):
    return jax.nn.silu(x)

def _sigmoid(x):
    return jax.nn.sigmoid(x)

def _layernorm(x, axis=-1, eps=1e-05):
    m = jnp.mean(x, axis=axis, keepdims=True)
    v = jnp.var(x, axis=axis, keepdims=True)
    return (x - m) / jnp.sqrt(v + eps)

def _scatter_add(tgt, idx, src, axis=0):
    return tgt.at[idx].add(src)

def _segment_sum(src, seg, n):
    return jax.ops.segment_sum(src, seg, n)
kernel_name = 'mk_seq_postln_d1_jaxref_r4_20a0b9'

def setup_inputs(seed: int=0):
    np.random.seed(seed)
    _w = jnp.asarray

    def _L0_attn_setup():
        import jax, jax.numpy as jnp
        import numpy as np
        HIDDEN = 512
        KEY = 512
        EPS = 1e-05
        key = jax.random.key(seed)
        k1, k2, k3 = jax.random.split(key, 3)
        B, S = (4, 512)
        x = jax.random.normal(k1, (B, S, HIDDEN), dtype=jnp.float32)
        bq = 1.0 / np.sqrt(HIDDEN)
        qkv = jax.random.uniform(k2, (HIDDEN, KEY * 3), minval=-bq, maxval=bq, dtype=jnp.float32)
        bo = 1.0 / np.sqrt(KEY)
        o_proj = jax.random.uniform(k3, (KEY, HIDDEN), minval=-bo, maxval=bo, dtype=jnp.float32)
        gamma = jnp.ones((HIDDEN,), dtype=jnp.float32)
        beta = jnp.zeros((HIDDEN,), dtype=jnp.float32)
        return {'x': x, 'qkv': qkv, 'o_proj': o_proj, 'gamma': gamma, 'beta': beta}
    _L0_attn_in = _L0_attn_setup()

    def _L0_ffn_setup():
        import jax, jax.numpy as jnp
        import numpy as np
        TOP_K = 2
        key = jax.random.key(seed)
        ks = jax.random.split(key, 5)
        B, S, D, INTER, E = (4, 512, 512, 512, 8)
        x = jax.random.normal(ks[0], (B, S, D), dtype=jnp.float32)
        w1 = jax.random.normal(ks[1], (INTER, D), dtype=jnp.float32) * (1.0 / np.sqrt(D))
        w3 = jax.random.normal(ks[2], (INTER, INTER), dtype=jnp.float32) * (1.0 / np.sqrt(INTER))
        w2 = jax.random.normal(ks[3], (D, INTER), dtype=jnp.float32) * (1.0 / np.sqrt(INTER))
        wr = jax.random.normal(ks[4], (E, D), dtype=jnp.float32) * (1.0 / np.sqrt(D))
        return {'x': x, 'w1': w1, 'w3': w3, 'w2': w2, 'wr': wr}
    _L0_ffn_in = _L0_ffn_setup()
    _d = {'L0_attn_x': _L0_attn_in['x'], 'L0_attn_qkv': _L0_attn_in['qkv'], 'L0_attn_o_proj': _L0_attn_in['o_proj'], 'L0_attn_gamma': _L0_attn_in['gamma'], 'L0_attn_beta': _L0_attn_in['beta'], 'L0_ffn_w1': _L0_ffn_in['w1'], 'L0_ffn_w3': _L0_ffn_in['w3'], 'L0_ffn_w2': _L0_ffn_in['w2'], 'L0_ffn_wr': _L0_ffn_in['wr']}
    _x0 = _d['L0_attn_x']
    _d['L0_attn_x'] = jax.random.normal(jax.random.fold_in(jax.random.key(seed), 1), (4, 2048, 512), dtype=_x0.dtype)
    del _x0
    return _d

def reference(L0_attn_x, L0_attn_qkv, L0_attn_o_proj, L0_attn_gamma, L0_attn_beta, L0_ffn_w1, L0_ffn_w3, L0_ffn_w2, L0_ffn_wr):

    def _L0_attn_ref(x, qkv, o_proj, gamma, beta):
        import jax, jax.numpy as jnp
        import numpy as np
        HIDDEN = 512
        KEY = 512
        EPS = 1e-05
        residual = x
        mu = jnp.mean(x, axis=-1, keepdims=True)
        var = jnp.mean((x - mu) ** 2, axis=-1, keepdims=True)
        x_norm = (x - mu) / jnp.sqrt(var + EPS) * gamma + beta
        q = x_norm @ qkv[:, :KEY]
        k = x_norm @ qkv[:, KEY:2 * KEY]
        v = x_norm @ qkv[:, 2 * KEY:]
        scale = 1.0 / jnp.sqrt(jnp.float32(KEY))
        scores = jnp.einsum('bsk,btk->bst', q, k) * scale
        S_len = x.shape[1]
        causal = jnp.tril(jnp.ones((S_len, S_len), dtype=bool))
        scores = jnp.where(causal[None], scores, -jnp.inf)
        attn = jax.nn.softmax(scores, axis=-1)
        out = attn @ v
        out = out @ o_proj
        return out + residual

    def _L0_ffn_ref(x, w1, w3, w2, wr):
        import jax, jax.numpy as jnp
        import numpy as np
        TOP_K = 2
        B, S, D = x.shape
        xr = x.reshape(-1, D)
        route_probs = jax.nn.softmax(xr @ wr.T, axis=-1)
        routes_k, indices_k = jax.lax.top_k(route_probs, TOP_K)
        gates = routes_k / jnp.sum(routes_k, axis=-1, keepdims=True)
        h = jax.nn.silu(xr @ w1.T)
        h = jax.nn.silu(h @ w3.T)
        h = h @ w2.T
        out = jnp.zeros_like(xr)
        for k in range(TOP_K):
            out = out.at[indices_k[:, k]].add(gates[:, k:k + 1] * h)
        return out.reshape(B, S, D)
    x = L0_attn_x
    x = _layernorm(x + _L0_attn_ref(x, L0_attn_qkv, L0_attn_o_proj, L0_attn_gamma, L0_attn_beta), axis=-1)
    x = _layernorm(x + _L0_ffn_ref(x, L0_ffn_w1, L0_ffn_w3, L0_ffn_w2, L0_ffn_wr), axis=-1)
    return x

_drawn_inputs = setup_inputs


def setup_inputs(seed=0):
    import zlib

    import numpy as np

    out = dict(_drawn_inputs(seed))
    spreads = {'L0_attn_gamma': (1.0, 0.6), 'L0_attn_beta': (0.0, 0.504)}
    factors = {'L0_attn_qkv': 3.067, 'L0_attn_o_proj': 2.912, 'L0_ffn_w1': 8.0, 'L0_ffn_wr': 8.0}
    for name, (base, spread) in spreads.items():
        noise = np.random.default_rng([zlib.crc32(name.encode()), seed]).standard_normal(out[name].shape)
        drawn = base * np.exp(spread * noise) if base else spread * noise
        out[name] = jnp.asarray(drawn.astype(out[name].dtype))
    for name, factor in factors.items():
        out[name] = (out[name] * factor).astype(out[name].dtype)
    return out
```

```python
from contextlib import ExitStack

import concourse.bass as bass
from concourse import mybir
from concourse.alu_op_type import AluOpType as ALU

F32 = mybir.dt.float32
F32R = mybir.dt.float32r
BF16 = mybir.dt.bfloat16
U32 = mybir.dt.uint32
ACT = mybir.ActivationFunctionType
AX = mybir.AxisListType

P = 128
D = 512
DC = D // P
EPS = 1e-5
MASKED = -3.0e38
E = 8
TOP_K = 2
DMA = 16


def attention_mlp(nc, x, wq_t, wk_t, wv_t, wo, gamma, beta, w1_t, w3_t, w2_t, wr_t, out):
    B, S = 4, x.shape[0] // 4
    TILES = S // P
    GROUP = 4
    GROUPS = TILES // GROUP
    SCALE = float(D) ** -0.5

    def chunks(t):
        return t // GROUP + 1

    def width(t, c):
        return GROUP * P if c < t // GROUP else (t % GROUP + 1) * P

    BEFORE = [sum(chunks(u) for u in range(t)) for t in range(TILES + 1)]
    CHUNKS = BEFORE[TILES]

    x1_scratch = nc.dram_tensor("x1_scratch", [B * S, D], F32, kind="Internal").ap()

    with ExitStack() as whole:
        def sb(name, shape, dt=F32, ctx=whole):
            return ctx.enter_context(nc.sbuf_tensor(name, shape, dt))

        def sem(name):
            return whole.enter_context(nc.semaphore(name))

        psum = whole.enter_context(nc.psum_tensor("psum", [P, 8, 512], F32))

        ident = sb("ident", [P, P])
        ident_bf = sb("ident_bf", [P, P], BF16)
        mask_bf = sb("mask_bf", [P, P], BF16)
        unused = sb("unused", [P, 1])
        minus_half = sb("minus_half", [P, 1])
        gamma_sb = sb("gamma_sb", [P, DC])
        beta_sb = sb("beta_sb", [P, DC])

        stage01 = ExitStack()
        whole.enter_context(stage01)
        m_hi = sb("m_hi", [P, DC, D], F32R, stage01)
        m_lo = sb("m_lo", [P, DC, D], F32R, stage01)
        wvo_hi = sb("wvo_hi", [P, DC, D], F32R, stage01)
        wvo_lo = sb("wvo_lo", [P, DC, D], F32R, stage01)

        setup = ExitStack()
        raw = [sb(f"raw{i}", [P, DC, D], F32, setup) for i in range(4)]
        raw_hi = [sb(f"raw_hi{i}", [P, DC, D], F32R, setup) for i in range(4)]
        raw_lo = [sb(f"raw_lo{i}", [P, DC, D], F32R, setup) for i in range(4)]
        setup.close()

        xt_hi = sb("xt_hi", [P, DC, S], F32R, stage01)
        xt_lo = sb("xt_lo", [P, DC, S], F32R, stage01)
        v_hi = sb("v_hi", [P, TILES, D], F32R, stage01)
        v_lo = sb("v_lo", [P, TILES, D], F32R, stage01)
        g_hi = sb("g_hi", [P, DC, GROUP * P], F32R, stage01)
        g_lo = sb("g_lo", [P, DC, GROUP * P], F32R, stage01)
        probs = sb("probs", [P, S], F32, stage01)
        pt_hi = sb("pt_hi", [P, 2, GROUP * P], F32R, stage01)
        pt_lo = sb("pt_lo", [P, 2, GROUP * P], F32R, stage01)
        xin = sb("xin", [P, 2, D], F32, stage01)
        affine = sb("affine", [P, 512], F32, stage01)
        tok = sb("tok", [P, 2, D], F32, stage01)
        outb = sb("outb", [P, D], F32, stage01)
        rowmax4 = sb("rowmax4", [P, 4], F32, stage01)
        rowmax = sb("rowmax", [P, 1], F32, stage01)
        bias = sb("bias", [P, 2], F32, stage01)
        sums4 = sb("sums4", [P, 2, 4], F32, stage01)
        rowsum = sb("rowsum", [P, 1], F32, stage01)
        rinv = sb("rinv", [P, 2], F32, stage01)
        stats = sb("stats", [P, 6], F32, stage01)
        meanvar = sb("meanvar", [P, 2], F32, stage01)
        var_eps = sb("var_eps", [P, 1], F32, stage01)
        rstd = sb("rstd", [P, 1], F32, stage01)
        stage01.close()

        TURN0 = 4
        ATTN = 6
        XBANK = 7

        consts_memset = sem("consts_memset")
        consts_ready = sem("consts_ready")
        half_ready = sem("half_ready")
        affine_loaded = sem("affine_loaded")
        weights_loaded = [sem(f"weights_loaded{i}") for i in range(4)]
        weights_hi = sem("weights_hi")
        weights_split = sem("weights_split")
        fold_done = sem("fold_done")
        fold_hi = sem("fold_hi")
        fold_split = sem("fold_split")

        x_loaded = [sem(f"x_loaded{i}") for i in range(2)]
        x_normed = sem("x_normed")
        x_turned = sem("x_turned")
        xt_hi_ready = sem("xt_hi_ready")
        xt_ready = sem("xt_ready")
        g_projected = sem("g_projected")
        g_hi_ready = sem("g_hi_ready")
        g_ready = sem("g_ready")
        v_projected = sem("v_projected")
        v_hi_ready = sem("v_hi_ready")
        v_ready = sem("v_ready")
        scores_ready = sem("scores_ready")
        bias_ready = sem("bias_ready")
        probs_ready = sem("probs_ready")
        probs_turned = sem("probs_turned")
        pt_hi_ready = sem("pt_hi_ready")
        pt_ready = sem("pt_ready")
        pv_done = sem("pv_done")
        res_loaded = [sem(f"res_loaded{i}") for i in range(2)]
        res_doubled = sem("res_doubled")
        attn_read = sem("attn_read")
        x1_ready = sem("x1_ready")
        x1_stored = [sem(f"x1_stored{i}") for i in range(2)]
        out_ready = sem("out_ready")
        out_stored = sem("out_stored")
        variance_ready = sem("variance_ready")
        rstd_ready = sem("rstd_ready")
        own = sem("own")

        XUNITS = 4
        NORMS = 3 * TILES

        def turn_bank(n):
            return TURN0 + n % 2

        def turn_use(t, c):
            return BEFORE[t] + c + GROUP * (1 + (t // GROUP))

        def v_use(g, j):
            return (BEFORE[GROUP * g] if g else 0) + GROUP * g + j

        NG = B * S // (GROUP * P)
        stage2 = ExitStack()
        whole.enter_context(stage2)
        w1_hi = sb("w1_hi", [P, DC, D], F32R, stage2)
        w1_lo = sb("w1_lo", [P, DC, D], F32R, stage2)
        w3_hi = sb("w3_hi", [P, DC, D], F32R, stage2)
        w3_lo = sb("w3_lo", [P, DC, D], F32R, stage2)
        w13_raw = sb("w13_raw", [P, 2, DC, D], F32, stage2)
        w2_sb = sb("w2_sb", [P, DC, D], F32, stage2)
        wr_raw = sb("wr_raw", [P, DC, E], F32, stage2)
        wr_s = sb("wr_s", [P, DC, P], F32R, stage2)
        x1_in = sb("x1_in", [P, 2, GROUP, D], F32, stage2)
        x1t_hi = sb("x1t_hi", [P, DC, GROUP * P], F32R, stage2)
        x1t_lo = sb("x1t_lo", [P, DC, GROUP * P], F32R, stage2)
        act_f = sb("act_f", [P, 2, D], F32, stage2)
        h1_hi = sb("h1_hi", [P, DC, GROUP * P], F32R, stage2)
        h1_lo = sb("h1_lo", [P, DC, GROUP * P], F32R, stage2)
        h2_hi = sb("h2_hi", [P, 2, D], F32R, stage2)
        h2_lo = sb("h2_lo", [P, 2, D], F32R, stage2)
        gates_s = sb("gates_s", [P, GROUP, P], F32R, stage2)
        logits_t = sb("logits_t", [P, GROUP * P], F32, stage2)
        fold = sb("fold", [P, P], F32, stage2)
        expert_f = sb("expert_f", [P, GROUP, E], F32, stage2)
        logits = sb("logits", [P, GROUP, E], F32, stage2)
        lmax = sb("lmax", [P, GROUP], F32, stage2)
        shifted = sb("shifted", [P, GROUP, E], F32, stage2)
        expo = sb("expo", [P, GROUP, E], F32, stage2)
        esum = sb("esum", [P, GROUP], F32, stage2)
        erec = sb("erec", [P, GROUP], F32, stage2)
        route = sb("route", [P, GROUP, E], F32, stage2)
        best = sb("best", [P, GROUP, 8], F32, stage2)
        best_at = sb("best_at", [P, GROUP, 8], U32, stage2)
        best_at_f = sb("best_at_f", [P, GROUP, 8], F32, stage2)
        chosen = sb("chosen", [P, TOP_K, GROUP, E], F32, stage2)
        picked = sb("picked", [P, GROUP, E], F32, stage2)
        kept = sb("kept", [P, GROUP, E], F32, stage2)
        ksum = sb("ksum", [P, GROUP], F32, stage2)
        krec = sb("krec", [P, GROUP], F32, stage2)
        gate_f = sb("gate_f", [P, GROUP, E], F32, stage2)
        acc_sb = sb("acc_sb", [P, D], F32, stage2)
        acc_t = sb("acc_t", [P, DC, P], F32, stage2)
        rows = sb("rows", [E, D], F32, stage2)
        rows_out = sb("rows_out", [E, D], F32, stage2)
        rstats = sb("rstats", [E, 6], F32, stage2)
        rmeanvar = sb("rmeanvar", [E, 2], F32, stage2)
        rvar_eps = sb("rvar_eps", [E, 1], F32, stage2)
        rrstd = sb("rrstd", [E, 1], F32, stage2)
        zero_r = sb("zero_r", [P, 512], F32R, stage2)

        LOGIT = 4
        LOGIT_T = 5
        ACC = 7
        FINAL = 6

        stage1_read = sem("stage1_read")
        fold_memset = sem("fold_memset")
        fold_ready = sem("fold_ready")
        iota_ready = sem("iota_ready")
        zeros_ready = sem("zeros_ready")
        w13_loaded = [sem(f"w13_loaded{i}") for i in range(2)]
        w2_loaded = sem("w2_loaded")
        wr_loaded = sem("wr_loaded")
        w13_hi = sem("w13_hi")
        w13_split = sem("w13_split")
        wr_hi = sem("wr_hi")
        wr_split = sem("wr_split")
        x1_loaded = [sem(f"x1_loaded{i}") for i in range(2)]
        x1_turned = sem("x1_turned")
        x1t_hi_ready = sem("x1t_hi_ready")
        x1t_ready = sem("x1t_ready")
        h1_product = sem("h1_product")
        h1_hi_ready = sem("h1_hi_ready")
        h1_ready = sem("h1_ready")
        h2_product = sem("h2_product")
        h2_hi_ready = sem("h2_hi_ready")
        h2_ready = sem("h2_ready")
        logits_product = sem("logits_product")
        logits_copied = sem("logits_copied")
        logits_turned = sem("logits_turned")
        logits_shifted = sem("logits_shifted")
        exp_ready = sem("exp_ready")
        gates_ready = sem("gates_ready")
        gated = sem("gated")
        rown = sem("rown")
        acc_done = sem("acc_done")
        acc_copied = sem("acc_copied")
        acc_turned = sem("acc_turned")
        acc_t_ready = sem("acc_t_ready")
        rows_product = sem("rows_product")
        rows_loaded = sem("rows_loaded")
        rows_variance = sem("rows_variance")
        rows_rstd = sem("rows_rstd")
        rows_ready = sem("rows_ready")
        rows_stored = sem("rows_stored")

        def split_product(pe, bank, ws, w_lo, ms, m_lo_, first, last, n=512):
            o = psum[:, bank, 0:n]
            pe.matmul(o, ws, ms, start=first, stop=False, skip_group_check=True)
            pe.matmul(o, w_lo, ms, start=False, stop=False, skip_group_check=True)
            return pe.matmul(o, ws, m_lo_, start=False, stop=last, skip_group_check=True)

        block = whole.enter_context(nc.Block())

        start_at_one = [*x1_stored, out_stored, xt_ready, xt_hi_ready, probs_turned, pv_done, probs_ready, pt_ready,
                        attn_read, h2_ready, h1_hi_ready, h2_hi_ready, gated, logits_copied]

        @block.sync
        def _(sp):
            for s in start_at_one:
                sp.sem_inc(s, 1)
            for i, w in enumerate((wq_t, wk_t, wv_t, wo)):
                sp.dma_start(raw[i][:], w.rearrange("(c p) n -> p c n", p=P)).then_inc(weights_loaded[i], DMA)
                if i == 1:
                    sp.dma_start(gamma_sb[:], gamma).then_inc(affine_loaded, DMA)
                    sp.dma_start(beta_sb[:], beta).then_inc(affine_loaded, DMA)
            with sp.Fori(0, B) as b:
                for t in range(TILES):
                    sp.wait_ge(x1_stored[t % 2], 1 + b * (TILES // 2 * DMA) + t // 2 * DMA)
                    sp.dma_start(tok[:, t % 2, :], x[bass.ds(b * S + t * P, P), :]).then_inc(res_loaded[t % 2], DMA)
                    if t >= 1:
                        rows_at = bass.ds(b * S + (t - 1) * P, P)
                        sp.wait_ge(x1_ready, b * TILES + t)
                        sp.dma_start(x1_scratch[rows_at, :], tok[:, (t - 1) % 2, :]).then_inc(x1_stored[(t - 1) % 2], DMA)
                        sp.wait_ge(out_ready, b * TILES + t)
                        sp.dma_start(out[rows_at, :], outb[:]).then_inc(out_stored, DMA)
                rows_at = bass.ds(b * S + (TILES - 1) * P, P)
                sp.wait_ge(x1_ready, b * TILES + TILES)
                sp.dma_start(x1_scratch[rows_at, :], tok[:, (TILES - 1) % 2, :]).then_inc(x1_stored[(TILES - 1) % 2], DMA)
                sp.wait_ge(out_ready, b * TILES + TILES)
                sp.dma_start(out[rows_at, :], outb[:]).then_inc(out_stored, DMA)

            for i in range(2):
                sp.wait_ge(x1_stored[i], 1 + B * TILES // 2 * DMA)
            sp.wait_ge(out_stored, 1 + B * TILES * DMA)
            sp.wait_ge(stage1_read, 3)
            for i, w in enumerate((w1_t, w3_t)):
                sp.dma_start(w13_raw[:, i], w.rearrange("(c p) n -> p c n", p=P)).then_inc(w13_loaded[i], DMA)
                sp.dma_start(x1_in[:, i], x1_scratch[i * 512:(i + 1) * 512, :].rearrange("(t p) d -> p t d", p=P)).then_inc(x1_loaded[i], DMA)
                if i == 0:
                    sp.dma_start(wr_raw[:], wr_t.rearrange("(c p) n -> p c n", p=P)).then_inc(wr_loaded, DMA)
            sp.dma_start(w2_sb[:], w2_t.rearrange("(c p) n -> p c n", p=P)).then_inc(w2_loaded, DMA)
            sp.dma_start(rows[:], x1_scratch[0:E, :]).then_inc(rows_loaded, DMA)
            with sp.Fori(1, NG // 2) as h:
                for s in range(2):
                    sp.wait_ge(x1_turned, (2 * h - 1 + s) * DC)
                    sp.dma_start(x1_in[:, s], x1_scratch[bass.ds((2 * h + s) * 512, 512), :].rearrange("(t p) d -> p t d", p=P)).then_inc(x1_loaded[s], DMA)
            sp.wait_ge(rows_ready, 1)
            sp.dma_start(out[0:E, :], rows_out[:]).then_inc(rows_stored, DMA)
            sp.wait_ge(rows_stored, DMA)

        @block.gpsimd
        def _(pool):
            pool.memset(ident[:], 0.0).then_inc(consts_memset, 1)
            pool.memset(ident_bf[:], 0.0).then_inc(consts_memset, 1)
            pool.memset(mask_bf[:], 0.0).then_inc(consts_memset, 1)
            pool.wait_ge(consts_memset, 3)
            for m in (ident, ident_bf):
                pool.affine_select(out=m[:], in_=m[:], compare_op=ALU.not_equal, fill=1.0, base=0,
                                   pattern=[[-1, P]], channel_multiplier=1).then_inc(consts_ready, 1)
            pool.affine_select(out=mask_bf[:], in_=mask_bf[:], compare_op=ALU.is_ge, fill=MASKED, base=0,
                               pattern=[[-1, P]], channel_multiplier=1).then_inc(consts_ready, 1)

            pool.memset(minus_half[:], -0.5).then_inc(half_ready, 1)
            pool.wait_ge(half_ready, 1)

            with pool.Fori(0, B) as b:
                count = [0]

                def inverse_root():
                    count[0] += 1
                    pool.wait_ge(variance_ready, b * NORMS + count[0])
                    pool.tensor_tensor(rstd[:], var_eps[:], minus_half[:], ALU.pow).then_inc(rstd_ready, 1)

                for _ in range(GROUP):
                    inverse_root()
                for t in range(TILES):
                    if t:
                        inverse_root()
                        inverse_root()
                    if t % GROUP < 2 and t // GROUP + 1 < GROUPS:
                        inverse_root()
                        inverse_root()
                    pool.wait_ge(res_loaded[t % 2], b * (TILES // 2 * DMA) + (t // 2 + 1) * DMA)
                    pool.tensor_tensor(tok[:, t % 2, :], tok[:, t % 2, :], tok[:, t % 2, :], ALU.add).then_inc(res_doubled, 1)
                inverse_root()
                inverse_root()
                assert count[0] == NORMS

            pool.wait_ge(stage1_read, 3)
            for i in range(2):
                pool.wait_ge(x1_stored[i], 1 + B * TILES // 2 * DMA)
            pool.wait_ge(out_stored, 1 + B * TILES * DMA)
            pool.memset(fold[:], 0.0).then_inc(fold_memset, 1)
            pool.wait_ge(fold_memset, 1)
            pool.affine_select(out=fold[:], in_=fold[:], compare_op=ALU.not_equal, fill=1.0, base=0,
                               pattern=[[-1, P]], channel_multiplier=1).then_inc(fold_memset, 1)
            pool.wait_ge(fold_memset, 2)
            pool.affine_select(out=fold[:], in_=fold[:], compare_op=ALU.not_equal, fill=1.0, base=-E,
                               pattern=[[-1, P]], channel_multiplier=1).then_inc(fold_ready, 1)
            pool.iota(expert_f[:], pattern=[[0, GROUP], [1, E]], base=0, channel_multiplier=0,
                      allow_small_or_imprecise_dtypes=True).then_inc(iota_ready, 1)
            pool.wait_ge(rows_variance, 1)
            pool.tensor_tensor(rrstd[:], rvar_eps[:], minus_half[0:E, :], ALU.pow).then_inc(rows_rstd, 1)

        @block.scalar
        def _(act):
            for i in range(4):
                act.wait_ge(weights_loaded[i], DMA)
                for c in range(DC):
                    act.activation(raw_hi[i][:, c, :], raw[i][:, c, :], ACT.Copy).then_inc(weights_hi, 1)
            for n in range(2 * DC):
                hi = m_hi if n < DC else wvo_hi
                act.wait_ge(fold_done, n + 1)
                act.activation(hi[:, n % DC, :], psum[:, n, :], ACT.Copy).then_inc(fold_hi, 1)
            act.wait_ge(affine_loaded, 2 * DMA)

            with act.Fori(0, B) as b:
                def load_x(pair):
                    for tile in (2 * pair, 2 * pair + 1):
                        act.dma_start(xin[:, tile % 2, :], x[bass.ds(b * S + tile * P, P), :]).then_inc(x_loaded[tile % 2], DMA)

                def turn_x(g, u):
                    n = g * XUNITS + u
                    at = (GROUP * g + 2 * (u // 2)) * P
                    act.wait_ge(xt_ready, 1 + b * (GROUPS * XUNITS) + n)
                    act.wait_ge(x_turned, b * (GROUPS * XUNITS) + n + 1)
                    for k in range(2):
                        c = 2 * (u % 2) + k
                        src = psum[:, XBANK, 256 * k:256 * (k + 1)]
                        act.activation(affine[:, 256 * k:256 * (k + 1)], src, ACT.Identity,
                                       bias=beta_sb[:, c:c + 1], scale=gamma_sb[:, c:c + 1])
                        last = act.activation(xt_hi[:, c, at:at + 256], src, ACT.Identity,
                                              bias=beta_sb[:, c:c + 1], scale=gamma_sb[:, c:c + 1])
                    last.then_inc(xt_hi_ready, 1)
                    if u % 2 == 1 and n // 2 + 1 < TILES // 2:
                        load_x(n // 2 + 1)

                def project_g(g):
                    for j in range(DC):
                        act.wait_ge(g_projected, b * (GROUPS * DC) + g * DC + j + 1)
                        act.activation(g_hi[:, j, :], psum[:, j, :], ACT.Copy).then_inc(g_hi_ready, 1)

                def project_v(g):
                    for j in range(GROUP):
                        act.wait_ge(v_projected, b * TILES + GROUP * g + j + 1)
                        act.activation(v_hi[:, GROUP * g + j, :], psum[:, turn_bank(v_use(g, j)), :], ACT.Copy).then_inc(v_hi_ready, 1)

                def exp(t, c):
                    if c == 0:
                        act.wait_ge(bias_ready, b * TILES + t + 1)
                    act.wait_ge(probs_turned, 1 + b * CHUNKS + (min(BEFORE[t - 1] + c + 1, BEFORE[t]) if t else 0))
                    w = width(t, c)
                    act.activation(probs[:, 512 * c:512 * c + w], psum[:, c, 0:w], ACT.Exp, bias=bias[:, t % 2:t % 2 + 1],
                                   scale=SCALE, accum_out=sums4[:, t % 2, c:c + 1]).then_inc(probs_ready, 1)

                def turn_probs(t, c):
                    n = BEFORE[t] + c
                    act.wait_ge(probs_turned, 1 + b * CHUNKS + n + 1)
                    act.wait_ge(pv_done, 1 + b * CHUNKS + max(n - 1, 0))
                    w = width(t, c)
                    act.activation(pt_hi[:, n % 2, 0:w], psum[:, turn_bank(turn_use(t, c)), 0:w], ACT.Copy).then_inc(pt_hi_ready, 1)

                load_x(0)
                for u in range(XUNITS):
                    turn_x(0, u)
                project_g(0)
                exp(0, 0)
                project_v(0)
                for t in range(TILES):
                    g, k = t // GROUP, t % GROUP
                    more = g + 1 < GROUPS
                    n_next = chunks(t + 1) if t + 1 < TILES else 0
                    turn_probs(t, 0)
                    if more and k == 1:
                        turn_x(g + 1, 1)
                    if more and k == 2:
                        turn_x(g + 1, 2)
                    for c in range(max(chunks(t), n_next)):
                        if c >= 1 and c < chunks(t):
                            turn_probs(t, c)
                        if more and k == 2 and c == chunks(t) - 1:
                            turn_x(g + 1, 3)
                        if c < n_next:
                            exp(t + 1, c)
                    if more and k == 0:
                        turn_x(g + 1, 0)
                    if more and k == 2:
                        project_g(g + 1)
                    if more and k == 3:
                        project_v(g + 1)
            act.drain().then_inc(stage1_read, 1)

            act.wait_ge(stage1_read, 3)
            for i in range(2):
                act.wait_ge(w13_loaded[i], DMA)
                for c in range(DC):
                    act.activation((w1_hi, w3_hi)[i][:, c, :], w13_raw[:, i, c, :], ACT.Copy).then_inc(w13_hi, 1)

            def turn_x1(i, c):
                act.wait_ge(x1_turned, i * DC + c + 1)
                act.activation(x1t_hi[:, c, :], psum[:, c, :], ACT.Copy).then_inc(x1t_hi_ready, 1)

            def silu(i, n, product, done, split, hi, slot_free=None):
                act.wait_ge(product, i * 4 + n + 1)
                act.activation(act_f[:, n % 2, :], psum[:, n, :], ACT.Silu)
                act.activation(hi, psum[:, n, :], ACT.Silu).then_inc(done, 1)

            def group(i, last):
                for n in range(DC):
                    if n < 2:
                        act.wait_ge(h2_ready, 1 + i * 4)
                    else:
                        act.wait_ge(h1_ready, i * 4 + n - 1)
                    silu(i, n, h1_product, h1_hi_ready, None, h1_hi[:, n, :])
                act.wait_ge(logits_product, i + 1)
                act.activation(logits_t[:], psum[:, LOGIT, :], ACT.Copy).then_inc(logits_copied, 1)
                if not last:
                    turn_x1(i + 1, 0)
                    turn_x1(i + 1, 1)
                act.wait_ge(logits_shifted, i + 1)
                act.activation(expo[:], shifted[:], ACT.Exp).then_inc(exp_ready, 1)
                for n in range(GROUP):
                    if n < 2:
                        act.wait_ge(h1_ready, i * 4 + 3 + n)
                    else:
                        act.wait_ge(h2_ready, 1 + i * 4 + n - 1)
                        act.wait_ge(gated, 1 + i * 4 + n - 1)
                    silu(i, n, h2_product, h2_hi_ready, None, h2_hi[:, n % 2, :])
                if not last:
                    turn_x1(i + 1, 2)
                    turn_x1(i + 1, 3)

            for c in range(DC):
                turn_x1(0, c)
            with act.Fori(0, NG - 1) as i:
                group(i, False)
            group(NG - 1, True)
            act.wait_ge(acc_done, 1)
            act.activation(acc_sb[:], psum[:, ACC, :], ACT.Copy).then_inc(acc_copied, 1)
            for c in range(DC):
                act.wait_ge(acc_turned, c + 1)
                act.activation(acc_t[:, c, :], psum[:, c, 0:P], ACT.Copy).then_inc(acc_t_ready, 1)

        @block.vector
        def _(dve):
            def carry_wait():
                dve.memset(unused[:], 0.0)

            for i in range(4):
                for c in range(DC):
                    dve.wait_ge(weights_hi, i * DC + c + 1)
                    dve.tensor_tensor(raw_lo[i][:, c, :], raw[i][:, c, :], raw_hi[i][:, c, :], ALU.subtract).then_inc(weights_split, 1)
            for n in range(2 * DC):
                hi, lo = (m_hi, m_lo) if n < DC else (wvo_hi, wvo_lo)
                dve.wait_ge(fold_hi, n + 1)
                dve.tensor_tensor(lo[:, n % DC, :], psum[:, n, :], hi[:, n % DC, :], ALU.subtract).then_inc(fold_split, 1)

            OWN = 2 * NORMS + TILES * 3 + (TILES - GROUP)

            with dve.Fori(0, B) as b:
                count, norms = [0], [0]

                def mine(instruction):
                    instruction.then_inc(own, 1)
                    count[0] += 1
                    dve.wait_ge(own, b * OWN + count[0])

                def statistics(rows_):
                    mine(dve.bn_stats(stats[:], rows_))
                    carry_wait()
                    mine(dve.bn_aggr(meanvar[:], stats[:]))
                    dve.tensor_scalar(var_eps[:], meanvar[:, 1:2], EPS, None, ALU.add).then_inc(variance_ready, 1)
                    norms[0] += 1
                    dve.wait_ge(rstd_ready, b * NORMS + norms[0])

                def normalised(o, rows_):
                    return dve.tensor_scalar(o, rows_, meanvar[:, 0:1], rstd[:], ALU.subtract, ALU.mult)

                def norm_x(tile):
                    dve.wait_ge(x_loaded[tile % 2], b * (TILES // 2 * DMA) + (tile // 2 + 1) * DMA)
                    statistics(xin[:, tile % 2, :])
                    normalised(xin[:, tile % 2, :], xin[:, tile % 2, :]).then_inc(x_normed, 1)

                def split_x(g, u):
                    at = (GROUP * g + 2 * (u // 2)) * P
                    c = 2 * (u % 2)
                    dve.wait_ge(xt_hi_ready, 1 + b * (GROUPS * XUNITS) + g * XUNITS + u + 1)
                    dve.tensor_tensor(xt_lo[:, c:c + 2, at:at + 256], affine[:].rearrange("p (k n) -> p k n", k=2),
                                      xt_hi[:, c:c + 2, at:at + 256], ALU.subtract).then_inc(xt_ready, 1)

                def split_g(g):
                    for j in range(DC):
                        dve.wait_ge(g_hi_ready, b * (GROUPS * DC) + g * DC + j + 1)
                        dve.tensor_tensor(g_lo[:, j, :], psum[:, j, :], g_hi[:, j, :], ALU.subtract).then_inc(g_ready, 1)

                def split_v(g):
                    for j in range(GROUP):
                        dve.wait_ge(v_hi_ready, b * TILES + GROUP * g + j + 1)
                        dve.tensor_tensor(v_lo[:, GROUP * g + j, :], psum[:, turn_bank(v_use(g, j)), :],
                                          v_hi[:, GROUP * g + j, :], ALU.subtract).then_inc(v_ready, 1)

                def split_probs(t, c):
                    n, w = BEFORE[t] + c, width(t, c)
                    dve.wait_ge(pt_hi_ready, b * CHUNKS + n + 1)
                    dve.tensor_tensor(pt_lo[:, n % 2, 0:w], psum[:, turn_bank(turn_use(t, c)), 0:w],
                                      pt_hi[:, n % 2, 0:w], ALU.subtract).then_inc(pt_ready, 1)

                def chunk_max(t, c):
                    dve.wait_ge(scores_ready, b * CHUNKS + BEFORE[t] + c + 1)
                    return dve.tensor_reduce((rowmax if chunks(t) == 1 else rowmax4)[:, c:c + 1], psum[:, c, 0:width(t, c)], AX.X, ALU.max)

                def row_bias(t):
                    mine(chunk_max(t, chunks(t) - 1))
                    if chunks(t) > 1:
                        mine(dve.tensor_reduce(rowmax[:], rowmax4[:, 0:chunks(t)], AX.X, ALU.max))
                    dve.tensor_scalar(bias[:, t % 2:t % 2 + 1], rowmax[:], -SCALE, None, ALU.mult).then_inc(bias_ready, 1)

                def row_sum(t):
                    dve.wait_ge(probs_ready, 1 + b * CHUNKS + BEFORE[t + 1])
                    mine(dve.tensor_reduce(rowsum[:], sums4[:, t % 2, 0:chunks(t)], AX.X, ALU.add))
                    mine(dve.reciprocal(rinv[:, t % 2:t % 2 + 1], rowsum[:]))

                def residual(t):
                    dve.wait_ge(pv_done, 1 + b * CHUNKS + BEFORE[t + 1])
                    dve.wait_ge(res_doubled, b * TILES + t + 1)
                    y = tok[:, t % 2, :]
                    dve.scalar_tensor_tensor(out=y, in0=psum[:, ATTN, :], scalar=rinv[:, t % 2:t % 2 + 1], in1=y,
                                             op0=ALU.mult, op1=ALU.add).then_inc(attn_read, 1)

                def layernorm1(t):
                    dve.wait_ge(attn_read, 1 + b * TILES + t + 1)
                    y = tok[:, t % 2, :]
                    statistics(y)
                    normalised(y, y).then_inc(x1_ready, 1)

                def layernorm2(t):
                    dve.wait_ge(x1_ready, b * TILES + t + 1)
                    statistics(tok[:, t % 2, :])
                    dve.wait_ge(out_stored, 1 + b * (TILES * DMA) + t * DMA)
                    normalised(outb[:], tok[:, t % 2, :]).then_inc(out_ready, 1)

                norm_x(0)
                norm_x(1)
                split_x(0, 0)
                split_x(0, 1)
                norm_x(2)
                norm_x(3)
                split_x(0, 2)
                split_x(0, 3)
                split_g(0)
                row_bias(0)
                split_v(0)
                for t in range(TILES):
                    g, k = t // GROUP, t % GROUP
                    more = g + 1 < GROUPS
                    if t:
                        residual(t - 1)
                    if t + 1 < TILES:
                        for c in range(chunks(t + 1) - 1):
                            chunk_max(t + 1, c)
                    split_probs(t, 0)
                    if t + 1 < TILES:
                        row_bias(t + 1)
                    row_sum(t)
                    if more and k == 1:
                        split_x(g + 1, 1)
                    if more and k == 2:
                        split_x(g + 1, 2)
                    if t:
                        layernorm1(t - 1)
                    if chunks(t) > 1:
                        split_probs(t, 1)
                    if more and k == 2 and chunks(t) <= 2:
                        split_x(g + 1, 3)
                    if t:
                        layernorm2(t - 1)
                    for c in range(2, chunks(t)):
                        split_probs(t, c)
                        if more and k == 2 and c == chunks(t) - 1:
                            split_x(g + 1, 3)
                    if more and k == 0:
                        norm_x(GROUP * (g + 1))
                        norm_x(GROUP * (g + 1) + 1)
                        split_x(g + 1, 0)
                    if more and k == 1:
                        norm_x(GROUP * (g + 1) + 2)
                        norm_x(GROUP * (g + 1) + 3)
                    if more and k == 2:
                        split_g(g + 1)
                    if more and k == 3:
                        split_v(g + 1)
                residual(TILES - 1)
                layernorm1(TILES - 1)
                layernorm2(TILES - 1)
                assert count[0] == OWN and norms[0] == NORMS
            dve.drain().then_inc(stage1_read, 1)

            dve.wait_ge(stage1_read, 3)
            for i in range(2):
                dve.wait_ge(x1_stored[i], 1 + B * TILES // 2 * DMA)
            dve.wait_ge(out_stored, 1 + B * TILES * DMA)
            dve.memset(wr_s[:].bitcast(F32), 0.0).then_inc(zeros_ready, 1)
            dve.memset(gates_s[:].bitcast(F32), 0.0).then_inc(zeros_ready, 1)
            dve.memset(zero_r[:].bitcast(F32), 0.0).then_inc(zeros_ready, 1)
            dve.wait_ge(zeros_ready, 3)
            for i in range(2):
                for c in range(DC):
                    dve.wait_ge(w13_hi, i * DC + c + 1)
                    dve.tensor_tensor((w1_lo, w3_lo)[i][:, c, :], w13_raw[:, i, c, :], (w1_hi, w3_hi)[i][:, c, :],
                                      ALU.subtract).then_inc(w13_split, 1)
                if i == 0:
                    dve.wait_ge(wr_loaded, DMA)
                    dve.tensor_copy(wr_s[:, :, 0:E], wr_raw[:]).then_inc(wr_hi, 1)
                    dve.wait_ge(wr_hi, 1)
                    dve.tensor_tensor(wr_s[:, :, E:2 * E], wr_raw[:], wr_s[:, :, 0:E], ALU.subtract).then_inc(wr_split, 1)
                    for c in range(DC):
                        dve.wait_ge(x1t_hi_ready, c + 1)
                        dve.tensor_tensor(x1t_lo[:, c, :], psum[:, c, :], x1t_hi[:, c, :], ALU.subtract).then_inc(x1t_ready, 1)

            dve.wait_ge(iota_ready, 1)

            ROUTE = 14

            def group(i, last):
                count = [0]

                def mine(instruction):
                    instruction.then_inc(rown, 1)
                    count[0] += 1
                    dve.wait_ge(rown, i * ROUTE + count[0])

                def spread(a):
                    return a.unsqueeze(2).to_broadcast([P, GROUP, E])

                def split_x1(c):
                    dve.wait_ge(x1t_hi_ready, (i + 1) * DC + c + 1)
                    dve.tensor_tensor(x1t_lo[:, c, :], psum[:, c, :], x1t_hi[:, c, :], ALU.subtract).then_inc(x1t_ready, 1)

                def split_h2(n):
                    dve.wait_ge(h2_hi_ready, 1 + i * 4 + n + 1)
                    dve.tensor_tensor(h2_lo[:, n % 2, :], act_f[:, n % 2, :], h2_hi[:, n % 2, :], ALU.subtract).then_inc(h2_ready, 1)

                for n in range(DC):
                    dve.wait_ge(h1_hi_ready, 1 + i * 4 + n + 1)
                    dve.tensor_tensor(h1_lo[:, n, :], act_f[:, n % 2, :], h1_hi[:, n, :], ALU.subtract).then_inc(h1_ready, 1)
                if not last:
                    split_x1(0)
                    split_x1(1)
                dve.wait_ge(logits_turned, i + 1)
                mine(dve.tensor_copy(logits[:], psum[:, LOGIT_T, 0:GROUP * E].rearrange("p (t e) -> p t e", e=E)))
                mine(dve.tensor_reduce(lmax[:], logits[:], AX.X, ALU.max))
                dve.tensor_tensor(shifted[:], logits[:], spread(lmax[:]), ALU.subtract).then_inc(logits_shifted, 1)
                dve.wait_ge(exp_ready, i + 1)
                mine(dve.tensor_reduce(esum[:], expo[:], AX.X, ALU.add))
                mine(dve.reciprocal(erec[:], esum[:]))
                mine(dve.tensor_tensor(route[:], expo[:], spread(erec[:]), ALU.mult))
                carry_wait()
                for t in range(GROUP):
                    largest = dve.max(best[:, t, :], route[:, t, :])
                mine(largest)
                carry_wait()
                for t in range(GROUP):
                    at = dve.max_index(best_at[:, t, :], best[:, t, :], route[:, t, :])
                mine(at)
                mine(dve.tensor_copy(best_at_f[:], best_at[:]))
                for k in range(TOP_K):
                    one_hot = dve.tensor_tensor(chosen[:, k], expert_f[:], best_at_f[:, :, k:k + 1].to_broadcast([P, GROUP, E]), ALU.is_equal)
                mine(one_hot)
                mine(dve.tensor_tensor(picked[:], chosen[:, 0], chosen[:, 1], ALU.add))
                mine(dve.tensor_tensor(kept[:], route[:], picked[:], ALU.mult))
                mine(dve.tensor_reduce(ksum[:], kept[:], AX.X, ALU.add))
                mine(dve.reciprocal(krec[:], ksum[:]))
                dve.wait_ge(gated, 1 + i * 4)
                mine(dve.tensor_tensor(gate_f[:], kept[:], spread(krec[:]), ALU.mult))
                assert count[0] == ROUTE, count[0]
                dve.tensor_copy(gates_s[:, :, 0:E], gate_f[:]).then_inc(gates_ready, 1)
                dve.wait_ge(gates_ready, 2 * i + 1)
                dve.tensor_tensor(gates_s[:, :, E:2 * E], gate_f[:], gates_s[:, :, 0:E], ALU.subtract).then_inc(gates_ready, 1)
                for n in range(GROUP):
                    split_h2(n)
                if not last:
                    split_x1(2)
                    split_x1(3)

            with dve.Fori(0, NG - 1) as i:
                group(i, False)
            group(NG - 1, True)

            dve.wait_ge(rows_loaded, DMA)
            dve.wait_ge(rows_product, 1)
            done = NG * ROUTE
            dve.tensor_tensor(rows[:], rows[:], psum[0:E, FINAL, :], ALU.add).then_inc(rown, 1)
            dve.wait_ge(rown, done + 1)
            dve.bn_stats(rstats[:], rows[:]).then_inc(rown, 1)
            dve.wait_ge(rown, done + 2)
            dve.bn_aggr(rmeanvar[:], rstats[:]).then_inc(rown, 1)
            dve.wait_ge(rown, done + 3)
            dve.tensor_scalar(rvar_eps[:], rmeanvar[:, 1:2], EPS, None, ALU.add).then_inc(rows_variance, 1)
            dve.wait_ge(rows_rstd, 1)
            dve.tensor_scalar(rows_out[:], rows[:], rmeanvar[:, 0:1], rrstd[:], ALU.subtract, ALU.mult).then_inc(rows_ready, 1)

        @block.tensor
        def _(pe):
            for n in range(2 * DC):
                a, w = (0, 1) if n < DC else (2, 3)
                if n % DC == 0:
                    pe.wait_ge(weights_split, (w + 1) * DC)
                rows_at = slice(n % DC * P, (n % DC + 1) * P)
                for c in range(DC):
                    last = split_product(pe, n, raw_hi[a][:, c, rows_at], raw_lo[a][:, c, rows_at],
                                         raw_hi[w][:, c, :], raw_lo[w][:, c, :], c == 0, c == DC - 1)
                last.then_inc(fold_done, 1)
            pe.wait_ge(fold_split, 2 * DC)
            pe.wait_ge(consts_ready, 3)

            with pe.Fori(0, B) as b:
                def turn_x(g, u):
                    n = g * XUNITS + u
                    if u % 2 == 0:
                        pe.wait_ge(x_normed, b * TILES + n + 2)
                    pe.wait_ge(xt_hi_ready, 1 + b * (GROUPS * XUNITS) + n)
                    for k in range(2):
                        c = 2 * (u % 2) + k
                        for tile in range(2):
                            at = 256 * k + P * tile
                            last = pe.transpose(psum[:, XBANK, at:at + P], xin[:, tile, c * P:(c + 1) * P], ident[:])
                    last.then_inc(x_turned, 1)

                def project_g(g):
                    pe.wait_ge(xt_ready, 1 + b * (GROUPS * XUNITS) + (g + 1) * XUNITS)
                    pe.wait_ge(probs_ready, 1 + b * CHUNKS + BEFORE[GROUP * g])
                    at = slice(GROUP * g * P, GROUP * (g + 1) * P)
                    for j in range(DC):
                        cols = slice(j * P, (j + 1) * P)
                        for c in range(DC):
                            last = split_product(pe, j, m_hi[:, c, cols], m_lo[:, c, cols],
                                                 xt_hi[:, c, at], xt_lo[:, c, at], c == 0, c == DC - 1)
                        last.then_inc(g_projected, 1)

                def project_v(g):
                    for j in range(GROUP):
                        tile = GROUP * g + j
                        free_turn_bank(v_use(g, j))
                        at = slice(tile * P, (tile + 1) * P)
                        for c in range(DC):
                            last = split_product(pe, turn_bank(v_use(g, j)), xt_hi[:, c, at], xt_lo[:, c, at],
                                                 wvo_hi[:, c, :], wvo_lo[:, c, :], c == 0, c == DC - 1)
                        last.then_inc(v_projected, 1)

                def free_turn_bank(n):
                    n -= 2
                    if n < 0:
                        pe.wait_ge(pt_ready, 1 + b * CHUNKS)
                        return
                    for g in range(GROUPS):
                        if v_use(g, 0) <= n <= v_use(g, GROUP - 1):
                            pe.wait_ge(v_ready, b * TILES + GROUP * g + n - v_use(g, 0) + 1)
                            return
                    before = sum(GROUP for g in range(GROUPS) if v_use(g, 0) < n)
                    pe.wait_ge(pt_ready, 1 + b * CHUNKS + n - before + 1)

                def score(t, c):
                    if c == 0:
                        pe.wait_ge(g_ready, b * (GROUPS * DC) + (t // GROUP + 1) * DC)
                    pe.wait_ge(probs_ready, 1 + b * CHUNKS + (min(BEFORE[t - 1] + c + 1, BEFORE[t]) if t else 0))
                    w = width(t, c)
                    q = slice(t % GROUP * P, (t % GROUP + 1) * P)
                    keys = slice(512 * c, 512 * c + w)
                    for k in range(DC):
                        last = split_product(pe, c, g_hi[:, k, q], g_lo[:, k, q], xt_hi[:, k, keys], xt_lo[:, k, keys],
                                             k == 0, k == DC - 1, w)
                        if k == 0 and c == chunks(t) - 1:
                            pe.matmul(psum[:, c, w - P:w], ident_bf[:], mask_bf[:], start=False, stop=False, skip_group_check=True)
                    last.then_inc(scores_ready, 1)

                def turn_probs(t, c):
                    n = turn_use(t, c)
                    pe.wait_ge(probs_ready, 1 + b * CHUNKS + BEFORE[t] + c + 1)
                    free_turn_bank(n)
                    for k in range(width(t, c) // P):
                        last = pe.transpose(psum[:, turn_bank(n), k * P:(k + 1) * P],
                                            probs[:, 512 * c + k * P:512 * c + (k + 1) * P], ident[:])
                    last.then_inc(probs_turned, 1)

                def attend(t, c):
                    n = BEFORE[t] + c
                    if c == 0:
                        pe.wait_ge(attn_read, 1 + b * TILES + t)
                        if t % GROUP == 0:
                            pe.wait_ge(v_ready, b * TILES + t + GROUP)
                    pe.wait_ge(pt_ready, 1 + b * CHUNKS + n + 1)
                    blocks = width(t, c) // P
                    for k in range(blocks):
                        at = slice(k * P, (k + 1) * P)
                        key = GROUP * c + k
                        last = split_product(pe, ATTN, pt_hi[:, n % 2, at], pt_lo[:, n % 2, at], v_hi[:, key, :], v_lo[:, key, :],
                                             key == 0, c == chunks(t) - 1 and k == blocks - 1)
                    last.then_inc(pv_done, 1)

                for u in range(XUNITS):
                    turn_x(0, u)
                project_g(0)
                score(0, 0)
                project_v(0)
                for t in range(TILES):
                    g, k = t // GROUP, t % GROUP
                    more = g + 1 < GROUPS
                    if t + 1 < TILES:
                        for c in range(chunks(t + 1) - 1):
                            score(t + 1, c)
                    turn_probs(t, 0)
                    if t + 1 < TILES:
                        score(t + 1, chunks(t + 1) - 1)
                    if more and k == 1:
                        turn_x(g + 1, 1)
                    if more and k == 2:
                        turn_x(g + 1, 2)
                    for c in range(chunks(t)):
                        if c + 1 < chunks(t):
                            turn_probs(t, c + 1)
                        if more and k == 2 and c == chunks(t) - 1:
                            turn_x(g + 1, 3)
                        attend(t, c)
                    if more and k == 0:
                        turn_x(g + 1, 0)
                    if more and k == 2:
                        project_g(g + 1)
                    if more and k == 3:
                        project_v(g + 1)
            pe.drain().then_inc(stage1_read, 1)

            pe.wait_ge(stage1_read, 3)
            pe.wait_ge(zeros_ready, 3)
            pe.wait_ge(fold_ready, 1)
            pe.matmul(psum[:, ACC, :], zero_r[:, 0:P], zero_r[:], start=True, stop=False, skip_group_check=True)

            def turn_x1(i, c):
                for t in range(GROUP):
                    last = pe.transpose(psum[:, c, t * P:(t + 1) * P], slot_of(i)[:, t, c * P:(c + 1) * P], ident[:])
                last.then_inc(x1_turned, 1)

            slot = [0]

            def slot_of(i):
                return x1_in[:, slot[0]]

            def group(i, last_group, parity):
                for n in range(DC):
                    if n == 0:
                        pe.wait_ge(x1t_ready, (i + 1) * DC)
                        pe.wait_ge(h2_hi_ready, 1 + i * 4)
                        pe.wait_ge(h1_hi_ready, 1 + i * 4)
                    cols = slice(n * P, (n + 1) * P)
                    for c in range(DC):
                        last = split_product(pe, n, w1_hi[:, c, cols], w1_lo[:, c, cols], x1t_hi[:, c, :], x1t_lo[:, c, :], c == 0, c == DC - 1)
                    last.then_inc(h1_product, 1)
                pe.wait_ge(logits_copied, 1 + i)
                for c in range(DC):
                    pe.matmul(psum[:, LOGIT, :], wr_s[:, c, :], x1t_hi[:, c, :], start=(c == 0), stop=False)
                    last = pe.matmul(psum[:, LOGIT, :], wr_s[:, c, :], x1t_lo[:, c, :], start=False, stop=(c == DC - 1))
                last.then_inc(logits_product, 1)
                if not last_group:
                    slot[0] = 1 - parity
                    pe.wait_ge(x1_loaded[slot[0]], loads(i, parity))
                    for c in range(2):
                        pe.wait_ge(h1_hi_ready, 1 + i * 4 + c + 1)
                        turn_x1(i + 1, c)
                pe.wait_ge(logits_copied, 1 + i + 1)
                for t in range(GROUP):
                    last = pe.matmul(psum[:, LOGIT_T, t * E:(t + 1) * E], logits_t[:, t * P:(t + 1) * P], fold[:, 0:E], start=True, stop=True)
                last.then_inc(logits_turned, 1)

                def gate(n):
                    if n == 0:
                        pe.wait_ge(gates_ready, 2 * i + 2)
                    pe.wait_ge(h2_ready, 1 + i * 4 + n + 1)
                    pe.matmul(psum[:, ACC, :], gates_s[:, n, :], h2_hi[:, n % 2, :], start=False, stop=False, skip_group_check=True)
                    pe.matmul(psum[:, ACC, :], gates_s[:, n, :], h2_lo[:, n % 2, :], start=False, stop=False, skip_group_check=True).then_inc(gated, 1)

                for n in range(GROUP):
                    if n == 0:
                        pe.wait_ge(h1_ready, (i + 1) * 4)
                        if not last_group:
                            pe.wait_ge(x1t_ready, (i + 1) * DC + 2)
                    at = slice(n * P, (n + 1) * P)
                    for c in range(DC):
                        last = split_product(pe, n, h1_hi[:, c, at], h1_lo[:, c, at], w3_hi[:, c, :], w3_lo[:, c, :], c == 0, c == DC - 1)
                    last.then_inc(h2_product, 1)
                    if n:
                        gate(n - 1)
                if not last_group:
                    for c in range(2, 4):
                        pe.wait_ge(h2_hi_ready, 1 + i * 4 + c + 1)
                        turn_x1(i + 1, c)
                gate(GROUP - 1)

            pe.wait_ge(x1_loaded[0], DMA)
            for c in range(DC):
                turn_x1(0, c)
            pe.wait_ge(wr_split, 1)
            pe.wait_ge(w13_split, 2 * DC)
            with pe.Fori(0, NG // 2 - 1) as h:
                for parity in range(2):
                    def loads(i, parity_):
                        return h * DMA + (1 + parity_) * DMA
                    group(2 * h + parity, False, parity)

            def loads(i, parity_):
                return (NG // 2) * DMA
            group(NG - 2, False, 0)
            group(NG - 1, True, 1)
            pe.matmul(psum[:, ACC, :], zero_r[:, 0:P], zero_r[:], start=False, stop=True, skip_group_check=True).then_inc(acc_done, 1)

            pe.wait_ge(acc_copied, 1)
            pe.wait_ge(h2_hi_ready, 1 + NG * 4)
            for c in range(DC):
                pe.matmul(psum[:, c, 0:P], acc_sb[:, c * P:(c + 1) * P], fold[:], start=True, stop=True).then_inc(acc_turned, 1)
            pe.wait_ge(w2_loaded, DMA)
            for c in range(DC):
                pe.wait_ge(acc_t_ready, c + 1)
                last = pe.matmul(psum[:, FINAL, :], acc_t[:, c, :], w2_sb[:, c, :], start=(c == 0), stop=(c == DC - 1))
            last.then_inc(rows_product, 1)


def kernel(L0_attn_x, L0_attn_qkv, L0_attn_o_proj, L0_attn_gamma, L0_attn_beta, L0_ffn_w1, L0_ffn_w3, L0_ffn_w2, L0_ffn_wr):
    import numpy as np
    import concourse.bacc as bacc
    from concourse.bass_utils import run_bass_kernel_spmd

    x = np.asarray(L0_attn_x)
    qkv = np.asarray(L0_attn_qkv)
    arrays = {
        "x": x.reshape(-1, D),
        "wq_t": qkv[:, 0:D].T,
        "wk_t": qkv[:, D:2 * D].T,
        "wv_t": qkv[:, 2 * D:3 * D].T,
        "wo": np.asarray(L0_attn_o_proj),
        "gamma": np.asarray(L0_attn_gamma).reshape(DC, P).T,
        "beta": np.asarray(L0_attn_beta).reshape(DC, P).T,
        "w1_t": np.asarray(L0_ffn_w1).T,
        "w3_t": np.asarray(L0_ffn_w3).T,
        "w2_t": np.asarray(L0_ffn_w2).T,
        "wr_t": np.asarray(L0_ffn_wr).T,
    }
    arrays = {f"in_{k}": np.ascontiguousarray(a) for k, a in arrays.items()}
    nc = bacc.Bacc("TRN2", target_bir_lowering=False, num_devices=1)
    args = [nc.dram_tensor(k, a.shape, mybir.dt.from_np(a.dtype), kind="ExternalInput").ap() for k, a in arrays.items()]
    out = nc.dram_tensor("out_dram", arrays["in_x"].shape, F32, kind="ExternalOutput").ap()
    attention_mlp(nc, *args, out)
    r = run_bass_kernel_spmd(nc, [arrays], core_ids=[0])
    return r.results[0]["out_dram"].reshape(x.shape)
```

```python
from contextlib import ExitStack

import concourse.bass as bass
from concourse import mybir
from concourse.alu_op_type import AluOpType as ALU

F32 = mybir.dt.float32
F32R = mybir.dt.float32r
BF16 = mybir.dt.bfloat16
U32 = mybir.dt.uint32
ACT = mybir.ActivationFunctionType
AX = mybir.AxisListType

P = 128
D = 512
DC = D // P
EPS = 1e-5
MASKED = -3.0e38
E = 8
TOP_K = 2
DMA = 16


def attention_mlp(nc, x, wq_t, wk_t, wv_t, wo, gamma, beta, w1_t, w3_t, w2_t, wr_t, out):
    B, S = 4, x.shape[0] // 4
    TILES = S // P
    GROUP = 4
    GROUPS = TILES // GROUP
    SCALE = float(D) ** -0.5

    def chunks(t):
        return t // GROUP + 1

    def width(t, c):
        return GROUP * P if c < t // GROUP else (t % GROUP + 1) * P

    SLOTS = 3

    def uses(slot, tiles=TILES):
        return len(range(slot, tiles, SLOTS))

    BEFORE = [sum(chunks(u) for u in range(t)) for t in range(TILES + 1)]
    CHUNKS = BEFORE[TILES]

    x1_scratch = nc.dram_tensor("x1_scratch", [B * S, D], F32, kind="Internal").ap()

    with ExitStack() as whole:
        def sb(name, shape, dt=F32, ctx=whole):
            return ctx.enter_context(nc.sbuf_tensor(name, shape, dt))

        def sem(name):
            return whole.enter_context(nc.semaphore(name))

        psum = whole.enter_context(nc.psum_tensor("psum", [P, 8, 512], F32))

        ident = sb("ident", [P, P])
        ident_bf = sb("ident_bf", [P, P], BF16)
        mask_bf = sb("mask_bf", [P, P], BF16)
        unused = sb("unused", [P, 1])
        minus_half = sb("minus_half", [P, 2])
        gamma_sb = sb("gamma_sb", [P, DC])
        beta_sb = sb("beta_sb", [P, DC])

        stage01 = ExitStack()
        whole.enter_context(stage01)
        m_hi = sb("m_hi", [P, DC, D], F32R)
        m_lo = sb("m_lo", [P, DC, D], F32R)
        wvo_hi = sb("wvo_hi", [P, DC, D], F32R)
        wvo_lo = sb("wvo_lo", [P, DC, D], F32R)
        w1_hi, w1_lo, w3_hi, w3_lo = m_hi, m_lo, wvo_hi, wvo_lo
        xin = sb("xin", [P, 2, D])
        stats = sb("stats", [P, 2, 6])
        meanvar = sb("meanvar", [P, 2, 2])
        var_eps = sb("var_eps", [P, 2])
        rstd = sb("rstd", [P, 2])

        xt_hi = sb("xt_hi", [P, DC, S], F32R, stage01)
        xt_lo = sb("xt_lo", [P, DC, S], F32R, stage01)
        affine = sb("affine", [P, 512], F32, stage01)
        tok = sb("tok", [P, SLOTS, D], F32, stage01)
        outb = sb("outb", [P, D], F32, stage01)
        rowmax4 = sb("rowmax4", [P, 4], F32, stage01)
        rowmax = sb("rowmax", [P, 1], F32, stage01)
        bias = sb("bias", [P, 2], F32, stage01)
        sums4 = sb("sums4", [P, 2, 4], F32, stage01)
        rowsum = sb("rowsum", [P, 1], F32, stage01)
        rinv = sb("rinv", [P, 2], F32, stage01)

        setup = ExitStack()
        raw = [sb(f"raw{i}", [P, DC, D], F32, setup) for i in range(4)]
        raw_hi = [sb(f"raw_hi{i}", [P, DC, D], F32R, setup) for i in range(4)]
        raw_lo = [sb(f"raw_lo{i}", [P, DC, D], F32R, setup) for i in range(4)]
        setup.close()

        v_hi = sb("v_hi", [P, TILES, D], F32R, stage01)
        v_lo = sb("v_lo", [P, TILES, D], F32R, stage01)
        g_hi = sb("g_hi", [P, DC, GROUP * P], F32R, stage01)
        g_lo = sb("g_lo", [P, DC, GROUP * P], F32R, stage01)
        probs = sb("probs", [P, S], F32, stage01)
        pt_hi = sb("pt_hi", [P, 2, GROUP * P], F32R, stage01)
        pt_lo = sb("pt_lo", [P, 2, GROUP * P], F32R, stage01)
        stage01.close()

        TURN0 = 4
        ATTN = 6
        XBANK = 7

        consts_memset = sem("consts_memset")
        consts_ready = sem("consts_ready")
        half_ready = sem("half_ready")
        affine_loaded = sem("affine_loaded")
        weights_loaded = [sem(f"weights_loaded{i}") for i in range(4)]
        weights_hi = sem("weights_hi")
        weights_split = sem("weights_split")
        fold_done = sem("fold_done")
        fold_hi = sem("fold_hi")
        fold_split = sem("fold_split")

        x_loaded = [sem(f"x_loaded{i}") for i in range(2)]
        x_normed = sem("x_normed")
        x_turned = sem("x_turned")
        affine_ready = sem("affine_ready")
        xt_hi_ready = sem("xt_hi_ready")
        xt_ready = sem("xt_ready")
        g_projected = sem("g_projected")
        g_hi_ready = sem("g_hi_ready")
        g_ready = sem("g_ready")
        v_projected = sem("v_projected")
        v_hi_ready = sem("v_hi_ready")
        v_ready = sem("v_ready")
        scores_ready = sem("scores_ready")
        bias_ready = sem("bias_ready")
        probs_ready = sem("probs_ready")
        probs_turned = sem("probs_turned")
        pt_hi_ready = sem("pt_hi_ready")
        pt_ready = sem("pt_ready")
        pv_done = sem("pv_done")
        res_loaded = [sem(f"res_loaded{i}") for i in range(SLOTS)]
        res_doubled = sem("res_doubled")
        attn_read = sem("attn_read")
        x1_ready = sem("x1_ready")
        x1_stored = [sem(f"x1_stored{i}") for i in range(SLOTS)]
        out_ready = sem("out_ready")
        out_stored = sem("out_stored")
        variance_ready = sem("variance_ready")
        rstd_ready = sem("rstd_ready")
        own = sem("own")

        FIRST_NORMS = 3
        NORMS = TILES // 2 + TILES + 1
        XUNITS = 4
        def turn_bank(n):
            return TURN0 + n % 2

        def turn_use(t, c):
            return BEFORE[t] + c + GROUP * (1 + min((t + 1) // GROUP, GROUPS - 1))

        def v_use(g, j):
            return (BEFORE[GROUP * g - 1] if g else 0) + GROUP * g + j

        NG = B * S // (GROUP * P)
        stage2 = ExitStack()
        whole.enter_context(stage2)
        x1_in = sb("x1_in", [P, 2, GROUP, D], F32, stage2)
        x1t_hi = sb("x1t_hi", [P, DC, GROUP * P], F32R, stage2)
        x1t_lo = sb("x1t_lo", [P, DC, GROUP * P], F32R, stage2)
        h1_hi = sb("h1_hi", [P, DC, GROUP * P], F32R, stage2)
        h1_lo = sb("h1_lo", [P, DC, GROUP * P], F32R, stage2)
        wr_s = sb("wr_s", [P, DC, P], F32R, stage2)
        gates_s = sb("gates_s", [P, GROUP, P], F32R, stage2)
        h2_hi = sb("h2_hi", [P, 2, D], F32R, stage2)
        h2_lo = sb("h2_lo", [P, 2, D], F32R, stage2)
        wr_raw = sb("wr_raw", [P, DC, E], F32, stage2)
        taken = 2 * GROUP * D + 4 * DC * GROUP * P + DC * P + GROUP * P + 4 * D + DC * E
        sb("not_yet_free", [P, 2 * DC * S - taken + (2 + SLOTS) * D + 64], F32, stage2)
        act_f = sb("act_f", [P, 2, D], F32, stage2)
        logits_t = sb("logits_t", [P, GROUP * P], F32, stage2)
        fold_rows = sb("fold_rows", [P, P], F32, stage2)
        expert_f = sb("expert_f", [P, GROUP, E], F32, stage2)
        euler = sb("euler", [P, GROUP, E], F32, stage2)
        logits = sb("logits", [P, GROUP, E], F32, stage2)
        lmax = sb("lmax", [P, GROUP], F32, stage2)
        shifted = sb("shifted", [P, GROUP, E], F32, stage2)
        expo = sb("expo", [P, GROUP, E], F32, stage2)
        esum = sb("esum", [P, GROUP], F32, stage2)
        erec = sb("erec", [P, GROUP], F32, stage2)
        route = sb("route", [P, GROUP, E], F32, stage2)
        best = sb("best", [P, GROUP, 8], F32, stage2)
        best_at = sb("best_at", [P, GROUP, 8], U32, stage2)
        best_at_f = sb("best_at_f", [P, GROUP, 8], F32, stage2)
        chosen = sb("chosen", [P, TOP_K, GROUP, E], F32, stage2)
        picked = sb("picked", [P, GROUP, E], F32, stage2)
        kept = sb("kept", [P, GROUP, E], F32, stage2)
        ksum = sb("ksum", [P, GROUP], F32, stage2)
        krec = sb("krec", [P, GROUP], F32, stage2)
        gate_f = sb("gate_f", [P, GROUP, E], F32, stage2)
        w2_sb = sb("w2_sb", [P, DC, D], F32, stage2)
        acc_sb = sb("acc_sb", [P, D], F32, stage2)
        acc_t = sb("acc_t", [P, DC, P], F32, stage2)
        rows = sb("rows", [E, D], F32, stage2)
        rows_out = sb("rows_out", [E, D], F32, stage2)
        rstats = sb("rstats", [E, 6], F32, stage2)
        rmeanvar = sb("rmeanvar", [E, 2], F32, stage2)
        rvar_eps = sb("rvar_eps", [E, 1], F32, stage2)
        rrstd = sb("rrstd", [E, 1], F32, stage2)

        LOGIT = 4
        LOGIT_T = 5
        ACC = 7
        FINAL = 6

        fold_memset = sem("fold_memset")
        fold_ready = sem("fold_ready")
        euler_ready = sem("euler_ready")
        iota_ready = sem("iota_ready")
        zeros_ready = sem("zeros_ready")
        w13_loaded = [sem(f"w13_loaded{i}") for i in range(2)]
        w2_loaded = sem("w2_loaded")
        wr_loaded = sem("wr_loaded")
        w13_hi = sem("w13_hi")
        w13_split = sem("w13_split")
        wr_hi = sem("wr_hi")
        wr_split = sem("wr_split")
        x1_loaded = [sem(f"x1_loaded{i}") for i in range(2)]
        x1_turned = sem("x1_turned")
        x1t_hi_ready = sem("x1t_hi_ready")
        x1t_ready = sem("x1t_ready")
        h1_product = sem("h1_product")
        h1_hi_ready = sem("h1_hi_ready")
        h1_ready = sem("h1_ready")
        h2_product = sem("h2_product")
        h2_hi_ready = sem("h2_hi_ready")
        h2_ready = sem("h2_ready")
        logits_product = sem("logits_product")
        logits_copied = sem("logits_copied")
        logits_turned = sem("logits_turned")
        logits_shifted = sem("logits_shifted")
        exp_ready = sem("exp_ready")
        gates_ready = sem("gates_ready")
        gated = sem("gated")
        rown = sem("rown")
        acc_done = sem("acc_done")
        acc_copied = sem("acc_copied")
        acc_turned = sem("acc_turned")
        acc_t_ready = sem("acc_t_ready")
        rows_product = sem("rows_product")
        rows_loaded = sem("rows_loaded")
        rows_variance = sem("rows_variance")
        rows_rstd = sem("rows_rstd")
        rows_ready = sem("rows_ready")
        rows_stored = sem("rows_stored")

        def fold_bank(n):
            return n if n < 7 else 0

        def h2_bank(n):
            return (n + 2) % 4

        def split_product(pe, bank, ws, w_lo, ms, m_lo_, first, last, n=512):
            o = psum[:, bank, 0:n]
            pe.matmul(o, ws, ms, start=first, stop=False, skip_group_check=True)
            pe.matmul(o, w_lo, ms, start=False, stop=False, skip_group_check=True)
            return pe.matmul(o, ws, m_lo_, start=False, stop=last, skip_group_check=True)

        block = whole.enter_context(nc.Block())

        start_at_one = [*x1_stored, out_stored, xt_ready, affine_ready, probs_turned, pv_done, probs_ready, pt_ready,
                        attn_read, h2_ready, h1_hi_ready, h2_hi_ready, logits_copied]

        @block.sync
        def _(sp):
            for s in start_at_one:
                sp.sem_inc(s, 1)
            for i, w in enumerate((wq_t, wk_t, wv_t, wo)):
                sp.dma_start(raw[i][:], w.rearrange("(c p) n -> p c n", p=P)).then_inc(weights_loaded[i], DMA)
                if i == 1:
                    sp.dma_start(gamma_sb[:], gamma).then_inc(affine_loaded, DMA)
                    sp.dma_start(beta_sb[:], beta).then_inc(affine_loaded, DMA)
            with sp.Fori(0, B) as b:
                def store_x1(t):
                    sp.wait_ge(x1_ready, b * TILES + t + 1)
                    sp.dma_start(x1_scratch[bass.ds(b * S + t * P, P), :], tok[:, t % SLOTS, :]).then_inc(x1_stored[t % SLOTS], DMA)

                def store_out(t):
                    sp.wait_ge(out_ready, b * TILES + t + 1)
                    sp.dma_start(out[bass.ds(b * S + t * P, P), :], outb[:]).then_inc(out_stored, DMA)

                for t in range(TILES):
                    if t >= 2:
                        store_x1(t - 2)
                    if t >= 3:
                        store_out(t - 3)
                    slot = t % SLOTS
                    sp.wait_ge(x1_stored[slot], 1 + b * (uses(slot) * DMA) + t // SLOTS * DMA)
                    sp.dma_start(tok[:, slot, :], x[bass.ds(b * S + t * P, P), :]).then_inc(res_loaded[slot], DMA)
                store_x1(TILES - 2)
                store_out(TILES - 3)
                store_x1(TILES - 1)
                store_out(TILES - 2)
                store_out(TILES - 1)

            for i in range(SLOTS):
                sp.wait_ge(x1_stored[i], 1 + B * uses(i) * DMA)
            sp.wait_ge(out_stored, 1 + B * TILES * DMA)
            sp.wait_ge(pv_done, 1 + B * CHUNKS)
            sp.dma_start(w2_sb[:], w2_t.rearrange("(c p) n -> p c n", p=P)).then_inc(w2_loaded, DMA)
            sp.dma_start(rows[:], x1_scratch[0:E, :]).then_inc(rows_loaded, DMA)
            with sp.Fori(1, NG // 2) as h:
                for s in range(2):
                    sp.wait_ge(x1_turned, (2 * h - 1 + s) * DC)
                    sp.dma_start(x1_in[:, s], x1_scratch[bass.ds((2 * h + s) * 512, 512), :].rearrange("(t p) d -> p t d", p=P)).then_inc(x1_loaded[s], DMA)
            sp.wait_ge(rows_ready, 1)
            sp.dma_start(out[0:E, :], rows_out[:]).then_inc(rows_stored, DMA)
            sp.wait_ge(rows_stored, DMA)

        @block.gpsimd
        def _(pool):
            pool.memset(ident[:], 0.0).then_inc(consts_memset, 1)
            pool.memset(ident_bf[:], 0.0).then_inc(consts_memset, 1)
            pool.memset(mask_bf[:], 0.0).then_inc(consts_memset, 1)
            pool.wait_ge(consts_memset, 3)
            for m in (ident, ident_bf):
                pool.affine_select(out=m[:], in_=m[:], compare_op=ALU.not_equal, fill=1.0, base=0,
                                   pattern=[[-1, P]], channel_multiplier=1).then_inc(consts_ready, 1)
            pool.affine_select(out=mask_bf[:], in_=mask_bf[:], compare_op=ALU.is_ge, fill=MASKED, base=0,
                               pattern=[[-1, P]], channel_multiplier=1).then_inc(consts_ready, 1)

            pool.memset(minus_half[:], -0.5).then_inc(half_ready, 1)
            pool.wait_ge(half_ready, 1)

            def inverse_root(b, n, a=0, z=2):
                pool.wait_ge(variance_ready, FIRST_NORMS + b * NORMS + n)
                pool.tensor_tensor(rstd[:, a:z], var_eps[:, a:z], minus_half[:, 0:z - a], ALU.pow).then_inc(rstd_ready, 1)

            def batch(b, last):
                n = 0
                for t in range(TILES):
                    if t % GROUP == 1 and t < TILES - GROUP:
                        n += 1
                        inverse_root(b, n)
                    if t:
                        n += 1
                        inverse_root(b, n, 0, 2 if t > 1 else 1)
                    if (t % GROUP == 3 and t < TILES - 1 and not (last and t > TILES - 2 * GROUP)) or (t == TILES - 2 and not last):
                        n += 1
                        inverse_root(b, n)
                    slot = t % SLOTS
                    pool.wait_ge(res_loaded[slot], b * (uses(slot) * DMA) + (t // SLOTS + 1) * DMA)
                    pool.tensor_tensor(tok[:, slot, :], tok[:, slot, :], tok[:, slot, :], ALU.add).then_inc(res_doubled, 1)
                inverse_root(b, n + 1)
                if not last:
                    n += 1
                    inverse_root(b, n + 1)
                inverse_root(b, n + 2, 1, 2)
                assert last or n + 2 == NORMS

            for n in range(FIRST_NORMS):
                inverse_root(0, n + 1 - FIRST_NORMS)
            with pool.Fori(0, B - 1) as b:
                batch(b, False)
            batch(B - 1, True)

            pool.wait_ge(pv_done, 1 + B * CHUNKS)
            pool.memset(fold_rows[:], 0.0).then_inc(fold_memset, 1)
            pool.wait_ge(fold_memset, 1)
            pool.affine_select(out=fold_rows[:], in_=fold_rows[:], compare_op=ALU.not_equal, fill=1.0, base=0,
                               pattern=[[-1, P]], channel_multiplier=1).then_inc(fold_memset, 1)
            pool.wait_ge(fold_memset, 2)
            pool.affine_select(out=fold_rows[:], in_=fold_rows[:], compare_op=ALU.not_equal, fill=1.0, base=-E,
                               pattern=[[-1, P]], channel_multiplier=1).then_inc(fold_ready, 1)
            pool.iota(expert_f[:], pattern=[[0, GROUP], [1, E]], base=0, channel_multiplier=0,
                      allow_small_or_imprecise_dtypes=True).then_inc(iota_ready, 1)
            pool.memset(euler[:], 2.718281828459045).then_inc(euler_ready, 1)
            pool.wait_ge(euler_ready, 1)
            with pool.Fori(0, NG) as i:
                pool.wait_ge(logits_shifted, i + 1)
                pool.tensor_tensor(expo[:], euler[:], shifted[:], ALU.pow).then_inc(exp_ready, 1)
            pool.wait_ge(rows_variance, 1)
            pool.tensor_tensor(rrstd[:], rvar_eps[:], minus_half[0:E, 0:1], ALU.pow).then_inc(rows_rstd, 1)

        @block.scalar
        def _(act):
            def weights_to_hi(pair):
                for c in range(DC):
                    for i in (2 * pair, 2 * pair + 1):
                        act.wait_ge(weights_loaded[i], DMA)
                        act.activation(raw_hi[i][:, c, :], raw[i][:, c, :], ACT.Copy).then_inc(weights_hi, 1)

            def fold_to_hi(pair):
                for n in range(pair * DC, (pair + 1) * DC):
                    act.wait_ge(fold_done, n + 1)
                    act.activation((m_hi, wvo_hi)[pair][:, n % DC, :], psum[:, fold_bank(n), :], ACT.Copy).then_inc(fold_hi, 1)

            def load_x(b, pair):
                for slot in range(2):
                    act.dma_start(xin[:, slot, :], x[bass.ds(b * S + (2 * pair + slot) * P, P), :]).then_inc(x_loaded[slot], DMA)

            def turn_x(b, g, u, more=True):
                n = g * XUNITS + u
                act.wait_ge(xt_ready, 1 + b * (GROUPS * XUNITS) + n)
                act.wait_ge(x_turned, b * (GROUPS * XUNITS) + n + 1)
                for k in range(2):
                    c = 2 * (u % 2) + k
                    last = act.activation(affine[:, 256 * k:256 * (k + 1)], psum[:, XBANK, 256 * k:256 * (k + 1)],
                                          ACT.Identity, bias=beta_sb[:, c:c + 1], scale=gamma_sb[:, c:c + 1])
                last.then_inc(affine_ready, 1)
                if u % 2 == 1 and more:
                    if n // 2 + 1 < TILES // 2:
                        load_x(b, n // 2 + 1)
                    else:
                        load_x(b + 1, 0)

            def project_g(b, g):
                for j in range(DC):
                    act.wait_ge(g_projected, b * (GROUPS * DC) + g * DC + j + 1)
                    act.activation(g_hi[:, j, :], psum[:, j, :], ACT.Copy).then_inc(g_hi_ready, 1)

            def project_v(b, g):
                for j in range(GROUP):
                    act.wait_ge(v_projected, b * TILES + GROUP * g + j + 1)
                    act.activation(v_hi[:, GROUP * g + j, :], psum[:, turn_bank(v_use(g, j)), :], ACT.Copy).then_inc(v_hi_ready, 1)

            def exp(b, t, c):
                if c == 0:
                    act.wait_ge(bias_ready, b * TILES + t + 1)
                if t:
                    act.wait_ge(probs_turned, 1 + b * CHUNKS + min(BEFORE[t - 1] + c + 1, BEFORE[t]))
                w = width(t, c)
                act.activation(probs[:, 512 * c:512 * c + w], psum[:, c, 0:w], ACT.Exp, bias=bias[:, t % 2:t % 2 + 1],
                               scale=SCALE, accum_out=sums4[:, t % 2, c:c + 1]).then_inc(probs_ready, 1)

            def exp_first(b):
                act.wait_ge(bias_ready, (b + 1) * TILES + 1)
                act.wait_ge(probs_turned, 1 + b * CHUNKS + BEFORE[TILES - 1] + 1)
                w = width(0, 0)
                act.activation(probs[:, 0:w], psum[:, 0, 0:w], ACT.Exp, bias=bias[:, 0:1],
                               scale=SCALE, accum_out=sums4[:, 0, 0:1]).then_inc(probs_ready, 1)

            def turn_probs(b, t, c):
                n = BEFORE[t] + c
                act.wait_ge(probs_turned, 1 + b * CHUNKS + n + 1)
                act.wait_ge(pv_done, 1 + b * CHUNKS + max(n - 1, 0))
                w = width(t, c)
                act.activation(pt_hi[:, n % 2, 0:w], psum[:, turn_bank(turn_use(t, c)), 0:w], ACT.Copy).then_inc(pt_hi_ready, 1)

            def load_w13(j):
                for n in (j, j + 1):
                    w = (w1_t, w3_t)[n // DC]
                    act.dma_start(xin[:, n % 2, :], w[n % DC * P:(n % DC + 1) * P, :]).then_inc(w13_loaded[n % 2], DMA)

            def split_w13(j):
                for n in (j, j + 1):
                    act.wait_ge(w13_loaded[n % 2], (n // 2 + 1) * DMA)
                    act.activation((w1_hi, w3_hi)[n // DC][:, n % DC, :], xin[:, n % 2, :], ACT.Copy).then_inc(w13_hi, 1)

            def batch(b, last):
                for t in range(TILES):
                    g, k = t // GROUP, t % GROUP
                    more = g + 1 < GROUPS
                    n_next = chunks(t + 1) if t + 1 < TILES else 0
                    if more and k == 2:
                        turn_x(b, g + 1, 2)
                    turn_probs(b, t, 0)
                    if chunks(t) > 1:
                        turn_probs(b, t, 1)
                    if more and k == 0:
                        turn_x(b, g + 1, 0)
                    if t == TILES - 2 and not last:
                        turn_x(b + 1, 0, 0)
                    if t == TILES - 1 and not last:
                        turn_x(b + 1, 0, 2)
                    for c in range(max(chunks(t), n_next)):
                        if c >= 2 and c < chunks(t):
                            turn_probs(b, t, c)
                        if more and k == 2 and c == chunks(t) - 1:
                            turn_x(b, g + 1, 3, more=not (last and g + 2 == GROUPS))
                        if c < n_next:
                            exp(b, t + 1, c)
                        if c == 1 and t == TILES - 2 and not last:
                            turn_x(b + 1, 0, 1)
                        if c == 1 and t == TILES - 1 and not last:
                            turn_x(b + 1, 0, 3)
                        if c == 2 and t == TILES - 1 and not last:
                            project_g(b + 1, 0)
                    if more and k == 0:
                        turn_x(b, g + 1, 1)
                    if more and k == 2:
                        project_g(b, g + 1)
                        project_v(b, g + 1)
                    if t == TILES - 1 and not last:
                        exp_first(b)
                        project_v(b + 1, 0)
                    first = TILES - 1 - GROUP
                    if last and first <= t < TILES - 1:
                        split_w13(2 * (t - first))
                    if last and first - 1 <= t < TILES - 2:
                        if t >= first:
                            act.wait_ge(w13_split, 2 * (t - first) + 2)
                        load_w13(2 * (t - first) + 2)
                    if last and t == TILES - 2:
                        act.wait_ge(scores_ready, B * CHUNKS)
                        for i in range(SLOTS):
                            act.wait_ge(x1_stored[i], 1 + uses(i, 2 * GROUP) * DMA)
                        for i in range(2):
                            act.dma_start(x1_in[:, i], x1_scratch[i * 512:(i + 1) * 512, :].rearrange("(t p) d -> p t d", p=P)).then_inc(x1_loaded[i], DMA)
                        act.dma_start(wr_raw[:], wr_t.rearrange("(c p) n -> p c n", p=P)).then_inc(wr_loaded, DMA)

            load_x(0, 0)
            weights_to_hi(0)
            act.wait_ge(affine_loaded, 2 * DMA)
            turn_x(0, 0, 0)
            turn_x(0, 0, 1)
            weights_to_hi(1)
            fold_to_hi(0)
            turn_x(0, 0, 2)
            turn_x(0, 0, 3)
            fold_to_hi(1)
            project_g(0, 0)
            exp(0, 0, 0)
            project_v(0, 0)
            with act.Fori(0, B - 1) as b:
                batch(b, False)
            batch(B - 1, True)

            def turn_x1(i, c):
                act.wait_ge(x1_turned, i * DC + c + 1)
                act.activation(x1t_hi[:, c, :], psum[:, c, :], ACT.Copy).then_inc(x1t_hi_ready, 1)

            def silu(bank, n, hi, done):
                act.activation(act_f[:, n % 2, :], psum[:, bank, :], ACT.Silu)
                act.activation(hi, psum[:, bank, :], ACT.Silu).then_inc(done, 1)

            def group(i, last):
                for n in range(DC):
                    act.wait_ge(h1_product, i * 4 + n + 1)
                    if n < 2:
                        act.wait_ge(h2_ready, 1 + i * 4)
                    else:
                        act.wait_ge(h1_ready, i * 4 + n - 1)
                    silu(n, n, h1_hi[:, n, :], h1_hi_ready)
                if not last:
                    turn_x1(i + 1, 0)
                    turn_x1(i + 1, 1)
                for n in range(GROUP):
                    if n == 3 and not last:
                        turn_x1(i + 1, 2)
                        turn_x1(i + 1, 3)
                    act.wait_ge(h2_product, i * 4 + n + 1)
                    if n < 2:
                        act.wait_ge(h1_ready, i * 4 + 3 + n)
                    else:
                        act.wait_ge(h2_ready, 1 + i * 4 + n - 1)
                        act.wait_ge(gated, i * 4 + n)
                    silu(h2_bank(n), n, h2_hi[:, n % 2, :], h2_hi_ready)

            for c in range(DC):
                turn_x1(0, c)
            with act.Fori(0, NG - 1) as i:
                group(i, False)
            group(NG - 1, True)
            act.wait_ge(acc_done, 1)
            act.activation(acc_sb[:], psum[:, ACC, :], ACT.Copy).then_inc(acc_copied, 1)
            for c in range(DC):
                act.wait_ge(acc_turned, c + 1)
                act.activation(acc_t[:, c, :], psum[:, c, 0:P], ACT.Copy).then_inc(acc_t_ready, 1)

        @block.vector
        def _(dve):
            def carry_wait():
                dve.memset(unused[:], 0.0)

            def weights_to_lo(pair):
                for c in range(DC):
                    for k in range(2):
                        i = 2 * pair + k
                        dve.wait_ge(weights_hi, pair * 2 * DC + 2 * c + k + 1)
                        dve.tensor_tensor(raw_lo[i][:, c, :], raw[i][:, c, :], raw_hi[i][:, c, :], ALU.subtract).then_inc(weights_split, 1)

            def fold_to_lo(pair):
                hi, lo = ((m_hi, m_lo), (wvo_hi, wvo_lo))[pair]
                for n in range(pair * DC, (pair + 1) * DC):
                    dve.wait_ge(fold_hi, n + 1)
                    dve.tensor_tensor(lo[:, n % DC, :], psum[:, fold_bank(n), :], hi[:, n % DC, :], ALU.subtract).then_inc(fold_split, 1)

            FIRST_OWN = 2 * FIRST_NORMS + 1
            OWN = 2 * NORMS + TILES * 3 + (TILES - GROUP)
            count, norms = [0], [0]
            at_batch = [0]

            def mine(instruction):
                instruction.then_inc(own, 1)
                count[0] += 1
                dve.wait_ge(own, at_batch[0] * OWN + count[0])

            def statistics(a, z, rows_of):
                for s in range(a, z):
                    done = dve.bn_stats(stats[:, s, :], rows_of(s))
                mine(done)
                carry_wait()
                for s in range(a, z):
                    done = dve.bn_aggr(meanvar[:, s, :], stats[:, s, :])
                mine(done)
                dve.tensor_scalar(var_eps[:, a:z], meanvar[:, a:z, 1], EPS, None, ALU.add).then_inc(variance_ready, 1)
                norms[0] += 1

            def roots():
                dve.wait_ge(rstd_ready, at_batch[0] * NORMS + norms[0])

            def normalised(s, o, rows_):
                return dve.tensor_scalar(o, rows_, meanvar[:, s, 0:1], rstd[:, s:s + 1], ALU.subtract, ALU.mult)

            def norm_x(b, pair):
                for s in range(2):
                    dve.wait_ge(x_loaded[s], b * (TILES // 2 * DMA) + (pair + 1) * DMA)
                statistics(0, 2, lambda s: xin[:, s, :])
                roots()
                normalised(0, xin[:, 0, :], xin[:, 0, :])
                normalised(1, xin[:, 1, :], xin[:, 1, :]).then_inc(x_normed, 1)

            def split_x(b, g, u):
                at = (GROUP * g + 2 * (u // 2)) * P
                c = 2 * (u % 2)
                n = b * (GROUPS * XUNITS) + g * XUNITS + u + 1
                value = affine[:].rearrange("p (k n) -> p k n", k=2)
                dve.wait_ge(affine_ready, 1 + n)
                dve.tensor_copy(xt_hi[:, c:c + 2, at:at + 256], value).then_inc(xt_hi_ready, 1)
                dve.wait_ge(xt_hi_ready, n)
                dve.tensor_tensor(xt_lo[:, c:c + 2, at:at + 256], value, xt_hi[:, c:c + 2, at:at + 256],
                                  ALU.subtract).then_inc(xt_ready, 1)

            def split_g(b, g):
                for j in range(DC):
                    dve.wait_ge(g_hi_ready, b * (GROUPS * DC) + g * DC + j + 1)
                    dve.tensor_tensor(g_lo[:, j, :], psum[:, j, :], g_hi[:, j, :], ALU.subtract).then_inc(g_ready, 1)

            def split_v(b, g, tiles=(0, GROUP)):
                for j in range(*tiles):
                    dve.wait_ge(v_hi_ready, b * TILES + GROUP * g + j + 1)
                    dve.tensor_tensor(v_lo[:, GROUP * g + j, :], psum[:, turn_bank(v_use(g, j)), :],
                                      v_hi[:, GROUP * g + j, :], ALU.subtract).then_inc(v_ready, 1)

            def split_probs(b, t, c):
                n, w = BEFORE[t] + c, width(t, c)
                dve.wait_ge(pt_hi_ready, b * CHUNKS + n + 1)
                dve.tensor_tensor(pt_lo[:, n % 2, 0:w], psum[:, turn_bank(turn_use(t, c)), 0:w],
                                  pt_hi[:, n % 2, 0:w], ALU.subtract).then_inc(pt_ready, 1)

            def chunk_max(b, t, c):
                dve.wait_ge(scores_ready, b * CHUNKS + BEFORE[t] + c + 1)
                return dve.tensor_reduce((rowmax if chunks(t) == 1 else rowmax4)[:, c:c + 1], psum[:, c, 0:width(t, c)], AX.X, ALU.max)

            def row_bias(b, t):
                mine(chunk_max(b, t, chunks(t) - 1))
                if chunks(t) > 1:
                    mine(dve.tensor_reduce(rowmax[:], rowmax4[:, 0:chunks(t)], AX.X, ALU.max))
                dve.tensor_scalar(bias[:, t % 2:t % 2 + 1], rowmax[:], -SCALE, None, ALU.mult).then_inc(bias_ready, 1)

            def row_sum(b, t):
                dve.wait_ge(probs_ready, 1 + b * CHUNKS + BEFORE[t + 1])
                mine(dve.tensor_reduce(rowsum[:], sums4[:, t % 2, 0:chunks(t)], AX.X, ALU.add))
                mine(dve.reciprocal(rinv[:, t % 2:t % 2 + 1], rowsum[:]))

            def residual(b, t):
                dve.wait_ge(pv_done, 1 + b * CHUNKS + BEFORE[t + 1])
                dve.wait_ge(res_doubled, b * TILES + t + 1)
                y = tok[:, t % SLOTS, :]
                dve.scalar_tensor_tensor(out=y, in0=psum[:, ATTN, :], scalar=rinv[:, t % 2:t % 2 + 1], in1=y,
                                         op0=ALU.mult, op1=ALU.add).then_inc(attn_read, 1)

            def behind_statistics(b, t):
                if t < TILES:
                    dve.wait_ge(attn_read, 1 + b * TILES + t + 1)
                if t:
                    dve.wait_ge(x1_ready, b * TILES + t)
                statistics(0 if t < TILES else 1, 2 if t else 1, lambda s: tok[:, (t - s) % SLOTS, :])

            def behind_apply(b, t):
                roots()
                if t < TILES:
                    y = tok[:, t % SLOTS, :]
                    normalised(0, y, y).then_inc(x1_ready, 1)
                if t:
                    dve.wait_ge(out_stored, 1 + b * (TILES * DMA) + (t - 1) * DMA)
                    normalised(1, outb[:], tok[:, (t - 1) % SLOTS, :]).then_inc(out_ready, 1)

            def split_w13(j):
                for n in (j, j + 1):
                    dve.wait_ge(w13_hi, n + 1)
                    dve.tensor_tensor((w1_lo, w3_lo)[n // DC][:, n % DC, :], xin[:, n % 2, :], (w1_hi, w3_hi)[n // DC][:, n % DC, :],
                                      ALU.subtract).then_inc(w13_split, 1)

            def batch(b, last):
                at_batch[0] = b
                count[0], norms[0] = FIRST_OWN, FIRST_NORMS
                for t in range(TILES):
                    g, k = t // GROUP, t % GROUP
                    more = g + 1 < GROUPS
                    if more and k == 2:
                        split_x(b, g + 1, 2)
                    if t:
                        residual(b, t - 1)
                    if t + 1 < TILES:
                        for c in range(chunks(t + 1) - 1):
                            chunk_max(b, t + 1, c)
                    split_probs(b, t, 0)
                    if t + 1 < TILES:
                        row_bias(b, t + 1)
                    row_sum(b, t)
                    if chunks(t) > 1:
                        split_probs(b, t, 1)
                    if more and k == 0:
                        split_x(b, g + 1, 0)
                    if t == TILES - 2 and not last:
                        split_x(b + 1, 0, 0)
                    if t == TILES - 1 and not last:
                        split_x(b + 1, 0, 2)
                    if more and k == 1:
                        norm_x(b, 2 * (g + 1) + 1)
                    if t:
                        behind_statistics(b, t - 1)
                    if t == TILES - 2 and not last:
                        split_x(b + 1, 0, 1)
                    if t == TILES - 1 and not last:
                        split_x(b + 1, 0, 3)
                    if chunks(t) > 2:
                        split_probs(b, t, 2)
                    if t:
                        behind_apply(b, t - 1)
                    if t == TILES - 1 and not last:
                        split_g(b + 1, 0)
                    if t == TILES - 1 and last:
                        start_stage2()
                    if chunks(t) > 3:
                        split_probs(b, t, 3)
                    if more and k == 2:
                        split_x(b, g + 1, 3)
                        split_g(b, g + 1)
                        split_v(b, g + 1)
                    if more and k == 0:
                        split_x(b, g + 1, 1)
                    if k == 3 and g + 2 < GROUPS:
                        norm_x(b, 2 * (g + 2))
                    if k == 3 and g + 2 == GROUPS and not last:
                        norm_x(b + 1, 0)
                    if t == TILES - 2 and not last:
                        norm_x(b + 1, 1)
                    first = TILES - 1 - GROUP
                    if last and first <= t < TILES - 1:
                        split_w13(2 * (t - first))
                if last:
                    residual(b, TILES - 1)
                    split_first_x1()
                    behind_statistics(b, TILES - 1)
                    behind_apply(b, TILES - 1)
                else:
                    row_bias(b + 1, 0)
                    residual(b, TILES - 1)
                    behind_statistics(b, TILES - 1)
                    split_v(b + 1, 0, (0, 1))
                    behind_apply(b, TILES - 1)
                    split_v(b + 1, 0, (1, 2))
                    norm_x(b + 1, 2)
                    split_v(b + 1, 0, (2, 3))
                behind_statistics(b, TILES)
                behind_apply(b, TILES)
                if not last:
                    split_v(b + 1, 0, (3, 4))
                assert last or (count[0] == FIRST_OWN + OWN and norms[0] == FIRST_NORMS + NORMS)

            def start_stage2():
                dve.wait_ge(scores_ready, B * CHUNKS)
                dve.memset(wr_s[:].bitcast(F32), 0.0).then_inc(zeros_ready, 1)
                dve.memset(gates_s[:].bitcast(F32), 0.0).then_inc(zeros_ready, 1)
                dve.memset(h2_hi[:].bitcast(F32), 0.0).then_inc(zeros_ready, 1)
                dve.memset(h2_lo[:].bitcast(F32), 0.0).then_inc(zeros_ready, 1)
                dve.wait_ge(zeros_ready, 4)
                dve.wait_ge(wr_loaded, DMA)
                dve.tensor_copy(wr_s[:, :, 0:E], wr_raw[:]).then_inc(wr_hi, 1)
                dve.wait_ge(wr_hi, 1)
                dve.tensor_tensor(wr_s[:, :, E:2 * E], wr_raw[:], wr_s[:, :, 0:E], ALU.subtract).then_inc(wr_split, 1)

            def split_first_x1():
                for c in range(DC):
                    dve.wait_ge(x1t_hi_ready, c + 1)
                    dve.tensor_tensor(x1t_lo[:, c, :], psum[:, c, :], x1t_hi[:, c, :], ALU.subtract).then_inc(x1t_ready, 1)

            norm_x(0, 0)
            weights_to_lo(0)
            split_x(0, 0, 0)
            split_x(0, 0, 1)
            weights_to_lo(1)
            norm_x(0, 1)
            fold_to_lo(0)
            split_x(0, 0, 2)
            split_x(0, 0, 3)
            fold_to_lo(1)
            split_g(0, 0)
            row_bias(0, 0)
            norm_x(0, 2)
            split_v(0, 0)
            assert count[0] == FIRST_OWN and norms[0] == FIRST_NORMS
            with dve.Fori(0, B - 1) as b:
                batch(b, False)
            batch(B - 1, True)

            dve.wait_ge(iota_ready, 1)

            ROUTE = 14

            def group(i, last):
                count = [0]

                def mine(instruction):
                    instruction.then_inc(rown, 1)
                    count[0] += 1
                    dve.wait_ge(rown, i * ROUTE + count[0])

                def spread(a):
                    return a.unsqueeze(2).to_broadcast([P, GROUP, E])

                def split_x1(c):
                    dve.wait_ge(x1t_hi_ready, (i + 1) * DC + c + 1)
                    dve.tensor_tensor(x1t_lo[:, c, :], psum[:, c, :], x1t_hi[:, c, :], ALU.subtract).then_inc(x1t_ready, 1)

                def split_h2(n):
                    dve.wait_ge(h2_hi_ready, 1 + i * 4 + n + 1)
                    dve.tensor_tensor(h2_lo[:, n % 2, :], act_f[:, n % 2, :], h2_hi[:, n % 2, :], ALU.subtract).then_inc(h2_ready, 1)

                def split_h1(n):
                    dve.wait_ge(h1_hi_ready, 1 + i * 4 + n + 1)
                    dve.tensor_tensor(h1_lo[:, n, :], act_f[:, n % 2, :], h1_hi[:, n, :], ALU.subtract).then_inc(h1_ready, 1)

                dve.wait_ge(logits_product, i + 1)
                dve.tensor_copy(logits_t[:], psum[:, LOGIT, :]).then_inc(logits_copied, 1)
                split_h1(0)
                dve.wait_ge(logits_turned, i + 1)
                mine(dve.tensor_copy(logits[:], psum[:, LOGIT_T, 0:GROUP * E].rearrange("p (t e) -> p t e", e=E)))
                mine(dve.tensor_reduce(lmax[:], logits[:], AX.X, ALU.max))
                dve.tensor_tensor(shifted[:], logits[:], spread(lmax[:]), ALU.subtract).then_inc(logits_shifted, 1)
                split_h1(1)
                split_h1(2)
                dve.wait_ge(exp_ready, i + 1)
                mine(dve.tensor_reduce(esum[:], expo[:], AX.X, ALU.add))
                mine(dve.reciprocal(erec[:], esum[:]))
                mine(dve.tensor_tensor(route[:], expo[:], spread(erec[:]), ALU.mult))
                carry_wait()
                for t in range(GROUP):
                    largest = dve.max(best[:, t, :], route[:, t, :])
                mine(largest)
                carry_wait()
                for t in range(GROUP):
                    at = dve.max_index(best_at[:, t, :], best[:, t, :], route[:, t, :])
                mine(at)
                split_h1(3)
                mine(dve.tensor_copy(best_at_f[:], best_at[:]))
                for k in range(TOP_K):
                    one_hot = dve.tensor_tensor(chosen[:, k], expert_f[:], best_at_f[:, :, k:k + 1].to_broadcast([P, GROUP, E]), ALU.is_equal)
                mine(one_hot)
                mine(dve.tensor_tensor(picked[:], chosen[:, 0], chosen[:, 1], ALU.add))
                mine(dve.tensor_tensor(kept[:], route[:], picked[:], ALU.mult))
                mine(dve.tensor_reduce(ksum[:], kept[:], AX.X, ALU.add))
                mine(dve.reciprocal(krec[:], ksum[:]))
                dve.wait_ge(gated, i * 4 + 1)
                mine(dve.tensor_tensor(gate_f[:], kept[:], spread(krec[:]), ALU.mult))
                assert count[0] == ROUTE, count[0]
                dve.tensor_copy(gates_s[:, :, 0:E], gate_f[:]).then_inc(gates_ready, 1)
                dve.wait_ge(gates_ready, 2 * i + 1)
                dve.tensor_tensor(gates_s[:, :, E:2 * E], gate_f[:], gates_s[:, :, 0:E], ALU.subtract).then_inc(gates_ready, 1)
                if not last:
                    split_x1(0)
                    split_x1(1)
                for n in range(GROUP):
                    if n == 3 and not last:
                        split_x1(2)
                        split_x1(3)
                    split_h2(n)

            with dve.Fori(0, NG - 1) as i:
                group(i, False)
            group(NG - 1, True)

            dve.wait_ge(rows_loaded, DMA)
            dve.wait_ge(rows_product, 1)
            done = NG * ROUTE
            dve.tensor_tensor(rows[:], rows[:], psum[0:E, FINAL, :], ALU.add).then_inc(rown, 1)
            dve.wait_ge(rown, done + 1)
            dve.bn_stats(rstats[:], rows[:]).then_inc(rown, 1)
            dve.wait_ge(rown, done + 2)
            dve.bn_aggr(rmeanvar[:], rstats[:]).then_inc(rown, 1)
            dve.wait_ge(rown, done + 3)
            dve.tensor_scalar(rvar_eps[:], rmeanvar[:, 1:2], EPS, None, ALU.add).then_inc(rows_variance, 1)
            dve.wait_ge(rows_rstd, 1)
            dve.tensor_scalar(rows_out[:], rows[:], rmeanvar[:, 0:1], rrstd[:], ALU.subtract, ALU.mult).then_inc(rows_ready, 1)

        @block.tensor
        def _(pe):
            def fold_weights(pair, chunks_):
                a, w = 2 * pair, 2 * pair + 1
                for c in chunks_:
                    pe.wait_ge(weights_split, pair * 2 * DC + 2 * c + 2)
                    for n in range(DC):
                        rows_at = slice(n * P, (n + 1) * P)
                        last = split_product(pe, fold_bank(pair * DC + n), raw_hi[a][:, c, rows_at], raw_lo[a][:, c, rows_at],
                                             raw_hi[w][:, c, :], raw_lo[w][:, c, :], c == 0, c == DC - 1)
                        if c == DC - 1:
                            last.then_inc(fold_done, 1)

            def turn_x(b, g, u):
                n = g * XUNITS + u
                if u % 2 == 0:
                    pe.wait_ge(x_normed, b * (TILES // 2) + n // 2 + 1)
                pe.wait_ge(affine_ready, 1 + b * (GROUPS * XUNITS) + n)
                for k in range(2):
                    c = 2 * (u % 2) + k
                    for tile in range(2):
                        at = 256 * k + P * tile
                        last = pe.transpose(psum[:, XBANK, at:at + P], xin[:, tile, c * P:(c + 1) * P], ident[:])
                last.then_inc(x_turned, 1)

            def project_g(b, g):
                pe.wait_ge(probs_ready, 1 + b * CHUNKS + BEFORE[GROUP * g])
                at = slice(GROUP * g * P, GROUP * (g + 1) * P)
                for j in range(DC):
                    cols = slice(j * P, (j + 1) * P)
                    for c in range(DC):
                        if j == 0 and c % 2 == 0:
                            pe.wait_ge(xt_ready, 1 + b * (GROUPS * XUNITS) + g * XUNITS + 3 + c // 2)
                        last = split_product(pe, j, m_hi[:, c, cols], m_lo[:, c, cols],
                                             xt_hi[:, c, at], xt_lo[:, c, at], c == 0, c == DC - 1)
                    last.then_inc(g_projected, 1)

            def project_v(b, g):
                for j in range(GROUP):
                    tile = GROUP * g + j
                    free_turn_bank(b, v_use(g, j))
                    at = slice(tile * P, (tile + 1) * P)
                    for c in range(DC):
                        last = split_product(pe, turn_bank(v_use(g, j)), xt_hi[:, c, at], xt_lo[:, c, at],
                                             wvo_hi[:, c, :], wvo_lo[:, c, :], c == 0, c == DC - 1)
                    last.then_inc(v_projected, 1)

            def free_turn_bank(b, n):
                n -= 2
                if n < 0:
                    pe.wait_ge(pt_ready, 1 + b * CHUNKS)
                    return
                for g in range(GROUPS):
                    if v_use(g, 0) <= n <= v_use(g, GROUP - 1):
                        pe.wait_ge(v_ready, b * TILES + GROUP * g + n - v_use(g, 0) + 1)
                        return
                before = sum(GROUP for g in range(GROUPS) if v_use(g, 0) < n)
                pe.wait_ge(pt_ready, 1 + b * CHUNKS + n - before + 1)

            def score(b, t, c):
                pe.wait_ge(probs_ready, 1 + b * CHUNKS + (min(BEFORE[t - 1] + c + 1, BEFORE[t]) if t else 0))
                w = width(t, c)
                q = slice(t % GROUP * P, (t % GROUP + 1) * P)
                keys = slice(512 * c, 512 * c + w)
                for k in range(DC):
                    if c == 0 and t % GROUP == 0:
                        pe.wait_ge(g_ready, b * (GROUPS * DC) + (t // GROUP) * DC + k + 1)
                    last = split_product(pe, c, g_hi[:, k, q], g_lo[:, k, q], xt_hi[:, k, keys], xt_lo[:, k, keys],
                                         k == 0, k == DC - 1, w)
                    if k == 0 and c == chunks(t) - 1:
                        pe.matmul(psum[:, c, w - P:w], ident_bf[:], mask_bf[:], start=False, stop=False, skip_group_check=True)
                last.then_inc(scores_ready, 1)

            def turn_probs(b, t, c):
                n = turn_use(t, c)
                pe.wait_ge(probs_ready, 1 + b * CHUNKS + BEFORE[t] + c + 1)
                free_turn_bank(b, n)
                for k in range(width(t, c) // P):
                    last = pe.transpose(psum[:, turn_bank(n), k * P:(k + 1) * P],
                                        probs[:, 512 * c + k * P:512 * c + (k + 1) * P], ident[:])
                last.then_inc(probs_turned, 1)

            def attend(b, t, c):
                n = BEFORE[t] + c
                if c == 0:
                    pe.wait_ge(attn_read, 1 + b * TILES + t)
                    if t % GROUP == 0:
                        pe.wait_ge(v_ready, b * TILES + t + GROUP)
                pe.wait_ge(pt_ready, 1 + b * CHUNKS + n + 1)
                blocks = width(t, c) // P
                for k in range(blocks):
                    at = slice(k * P, (k + 1) * P)
                    key = GROUP * c + k
                    last = split_product(pe, ATTN, pt_hi[:, n % 2, at], pt_lo[:, n % 2, at], v_hi[:, key, :], v_lo[:, key, :],
                                         key == 0, c == chunks(t) - 1 and k == blocks - 1)
                last.then_inc(pv_done, 1)

            def batch(b, last):
                for t in range(TILES):
                    g, k = t // GROUP, t % GROUP
                    more = g + 1 < GROUPS
                    if more and k == 2:
                        turn_x(b, g + 1, 2)
                    if t + 1 < TILES:
                        for c in range(chunks(t + 1) - 1):
                            score(b, t + 1, c)
                    turn_probs(b, t, 0)
                    if t + 1 < TILES:
                        score(b, t + 1, chunks(t + 1) - 1)
                    if more and k == 0:
                        turn_x(b, g + 1, 0)
                    if t == TILES - 2 and not last:
                        turn_x(b + 1, 0, 0)
                    if t == TILES - 1 and not last:
                        turn_x(b + 1, 0, 2)
                    for c in range(chunks(t)):
                        if c + 1 < chunks(t):
                            turn_probs(b, t, c + 1)
                        if more and k == 2 and c == chunks(t) - 1:
                            turn_x(b, g + 1, 3)
                        if c == 1 and t == TILES - 2 and not last:
                            turn_x(b + 1, 0, 1)
                        if c == 1 and t == TILES - 1 and not last:
                            turn_x(b + 1, 0, 3)
                        attend(b, t, c)
                        if c == 1 and t == TILES - 1 and not last:
                            project_g(b + 1, 0)
                        if c == 2 and t == TILES - 1 and not last:
                            score(b + 1, 0, 0)
                    if more and k == 0:
                        turn_x(b, g + 1, 1)
                    if more and k == 2:
                        project_g(b, g + 1)
                        project_v(b, g + 1)
                if not last:
                    project_v(b + 1, 0)

            pe.wait_ge(consts_ready, 3)
            turn_x(0, 0, 0)
            turn_x(0, 0, 1)
            fold_weights(0, range(DC))
            turn_x(0, 0, 2)
            pe.wait_ge(fold_split, 1)
            fold_weights(1, range(2))
            turn_x(0, 0, 3)
            fold_weights(1, range(2, DC))
            pe.wait_ge(fold_split, 2 * DC)
            project_g(0, 0)
            score(0, 0, 0)
            project_v(0, 0)
            with pe.Fori(0, B - 1) as b:
                batch(b, False)
            batch(B - 1, True)

            def turn_x1(i, c):
                for t in range(GROUP):
                    last = pe.transpose(psum[:, c, t * P:(t + 1) * P], slot_of(i)[:, t, c * P:(c + 1) * P], ident[:])
                last.then_inc(x1_turned, 1)

            slot = [0]

            def slot_of(i):
                return x1_in[:, slot[0]]

            def gate(i, n, before=False):
                if n == 0:
                    pe.wait_ge(gates_ready, 2 * i + 2)
                pe.wait_ge(h2_ready, 1 + i * 4 + (0 if before else n + 1))
                pe.matmul(psum[:, ACC, :], gates_s[:, n, :], h2_hi[:, n % 2, :], start=False, stop=False, skip_group_check=True)
                pe.matmul(psum[:, ACC, :], gates_s[:, n, :], h2_lo[:, n % 2, :], start=False, stop=False, skip_group_check=True).then_inc(gated, 1)

            def group(i, last_group, parity):
                pe.wait_ge(logits_copied, 1 + i)
                for c in range(DC):
                    pe.wait_ge(x1t_ready, i * DC + c + 1)
                    pe.matmul(psum[:, LOGIT, :], wr_s[:, c, :], x1t_hi[:, c, :], start=(c == 0), stop=False)
                    last = pe.matmul(psum[:, LOGIT, :], wr_s[:, c, :], x1t_lo[:, c, :], start=False, stop=(c == DC - 1))
                last.then_inc(logits_product, 1)
                for n in range(DC):
                    if n < 2:
                        pe.wait_ge(h2_hi_ready, 1 + i * 4 - 1 + n)
                    cols = slice(n * P, (n + 1) * P)
                    for c in range(DC):
                        last = split_product(pe, n, w1_hi[:, c, cols], w1_lo[:, c, cols], x1t_hi[:, c, :], x1t_lo[:, c, :], c == 0, c == DC - 1)
                    last.then_inc(h1_product, 1)
                    if n == 0:
                        gate(i, 3, before=True)
                        pe.wait_ge(logits_copied, 1 + i + 1)
                        for t in range(GROUP):
                            last = pe.matmul(psum[:, LOGIT_T, t * E:(t + 1) * E], logits_t[:, t * P:(t + 1) * P], fold_rows[:, 0:E], start=True, stop=True)
                        last.then_inc(logits_turned, 1)
                if not last_group:
                    slot[0] = 1 - parity
                    pe.wait_ge(x1_loaded[slot[0]], loads(i, parity))
                    for c in range(2):
                        pe.wait_ge(h1_hi_ready, 1 + i * 4 + c + 1)
                        turn_x1(i + 1, c)
                for n in range(GROUP):
                    if n == 0:
                        pe.wait_ge(h1_hi_ready, 1 + i * 4 + 3)
                    if n == 2 and not last_group:
                        pe.wait_ge(x1t_ready, (i + 1) * DC + 2)
                    at = slice(n * P, (n + 1) * P)
                    for c in range(DC):
                        if n == 0:
                            pe.wait_ge(h1_ready, i * 4 + c + 1)
                        last = split_product(pe, h2_bank(n), h1_hi[:, c, at], h1_lo[:, c, at], w3_hi[:, c, :], w3_lo[:, c, :], c == 0, c == DC - 1)
                    last.then_inc(h2_product, 1)
                    if n == 2 and not last_group:
                        for c in (2, 3):
                            pe.wait_ge(h2_hi_ready, 1 + i * 4 + c - 1)
                            turn_x1(i + 1, c)
                    if n:
                        gate(i, n - 1)

            pe.wait_ge(x1_loaded[0], DMA)
            pe.wait_ge(probs_ready, 1 + B * CHUNKS)
            for c in range(DC):
                turn_x1(0, c)
            pe.wait_ge(zeros_ready, 4)
            pe.matmul(psum[:, ACC, :], gates_s[:, 0, :], h2_hi[:, 0, :], start=True, stop=False, skip_group_check=True)
            pe.wait_ge(fold_ready, 1)
            pe.wait_ge(wr_split, 1)
            pe.wait_ge(w13_split, 2 * DC)
            with pe.Fori(0, NG // 2 - 1) as h:
                for parity in range(2):
                    def loads(i, parity_):
                        return h * DMA + (1 + parity_) * DMA
                    group(2 * h + parity, False, parity)

            def loads(i, parity_):
                return (NG // 2) * DMA
            group(NG - 2, False, 0)
            group(NG - 1, True, 1)
            gate(NG - 1, 3)
            pe.drain().then_inc(acc_done, 1)

            pe.wait_ge(acc_copied, 1)
            pe.wait_ge(h2_hi_ready, 1 + NG * 4)
            for c in range(DC):
                pe.matmul(psum[:, c, 0:P], acc_sb[:, c * P:(c + 1) * P], fold_rows[:], start=True, stop=True).then_inc(acc_turned, 1)
            pe.wait_ge(w2_loaded, DMA)
            for c in range(DC):
                pe.wait_ge(acc_t_ready, c + 1)
                last = pe.matmul(psum[:, FINAL, :], acc_t[:, c, :], w2_sb[:, c, :], start=(c == 0), stop=(c == DC - 1))
            last.then_inc(rows_product, 1)


def kernel(L0_attn_x, L0_attn_qkv, L0_attn_o_proj, L0_attn_gamma, L0_attn_beta, L0_ffn_w1, L0_ffn_w3, L0_ffn_w2, L0_ffn_wr):
    import numpy as np
    import concourse.bacc as bacc
    from concourse.bass_utils import run_bass_kernel_spmd

    x = np.asarray(L0_attn_x)
    qkv = np.asarray(L0_attn_qkv)
    arrays = {
        "x": x.reshape(-1, D),
        "wq_t": qkv[:, 0:D].T,
        "wk_t": qkv[:, D:2 * D].T,
        "wv_t": qkv[:, 2 * D:3 * D].T,
        "wo": np.asarray(L0_attn_o_proj),
        "gamma": np.asarray(L0_attn_gamma).reshape(DC, P).T,
        "beta": np.asarray(L0_attn_beta).reshape(DC, P).T,
        "w1_t": np.asarray(L0_ffn_w1).T,
        "w3_t": np.asarray(L0_ffn_w3).T,
        "w2_t": np.asarray(L0_ffn_w2).T,
        "wr_t": np.asarray(L0_ffn_wr).T,
    }
    arrays = {f"in_{k}": np.ascontiguousarray(a) for k, a in arrays.items()}
    nc = bacc.Bacc("TRN2", target_bir_lowering=False, num_devices=1)
    args = [nc.dram_tensor(k, a.shape, mybir.dt.from_np(a.dtype), kind="ExternalInput").ap() for k, a in arrays.items()]
    out = nc.dram_tensor("out_dram", arrays["in_x"].shape, F32, kind="ExternalOutput").ap()
    attention_mlp(nc, *args, out)
    r = run_bass_kernel_spmd(nc, [arrays], core_ids=[0])
    return r.results[0]["out_dram"].reshape(x.shape)
```

```python
from contextlib import ExitStack

import concourse.bass as bass
from concourse import mybir
from concourse.alu_op_type import AluOpType as ALU

F32 = mybir.dt.float32
F32R = mybir.dt.float32r
BF16 = mybir.dt.bfloat16
U32 = mybir.dt.uint32
ACT = mybir.ActivationFunctionType
AX = mybir.AxisListType

P = 128
D = 512
DC = D // P
EPS = 1e-5
MASKED = -3.0e38
E = 8
TOP_K = 2
DMA = 16


def attention_mlp(nc, x, wq_t, wk_t, wv_t, wo, gamma, beta, w1_t, w3_t, w2_t, wr_t, out):
    B, S = 4, x.shape[0] // 4
    TILES = S // P
    GROUP = 4
    GROUPS = TILES // GROUP
    SCALE = float(D) ** -0.5

    def chunks(t):
        return t // GROUP + 1

    def key_start(t, c):
        return GROUP * P * c - (P if c == chunks(t) - 1 and t % GROUP == 0 and t else 0)

    def width(t, c):
        return (key_start(t, c + 1) if c + 1 < chunks(t) else (t + 1) * P) - key_start(t, c)

    SLOTS = 4
    USES = TILES // SLOTS

    BEFORE = [sum(chunks(u) for u in range(t)) for t in range(TILES + 1)]
    CHUNKS = BEFORE[TILES]

    x1_scratch = nc.dram_tensor("x1_scratch", [B * S, D], F32, kind="Internal").ap()

    with ExitStack() as whole:
        def sb(name, shape, dt=F32, ctx=whole):
            return ctx.enter_context(nc.sbuf_tensor(name, shape, dt))

        def sem(name):
            return whole.enter_context(nc.semaphore(name))

        psum = whole.enter_context(nc.psum_tensor("psum", [P, 8, 512], F32))

        ident = sb("ident", [P, P])
        ident_bf = sb("ident_bf", [P, P], BF16)
        mask_bf = sb("mask_bf", [P, P], BF16)
        unused = sb("unused", [P, 1])
        minus_half = sb("minus_half", [P, 2])
        gamma_sb = sb("gamma_sb", [P, DC])
        beta_sb = sb("beta_sb", [P, DC])

        stage01 = ExitStack()
        whole.enter_context(stage01)
        m_hi = sb("m_hi", [P, DC, D], F32R)
        m_lo = sb("m_lo", [P, DC, D], F32R)
        wvo_hi = sb("wvo_hi", [P, DC, D], F32R)
        wvo_lo = sb("wvo_lo", [P, DC, D], F32R)
        w1_hi, w1_lo, w3_hi, w3_lo = m_hi, m_lo, wvo_hi, wvo_lo
        xin = sb("xin", [P, 2, D])
        stats = sb("stats", [P, 4, 6])
        meanvar = sb("meanvar", [P, 4, 2])
        eps = sb("eps", [P, 2])
        minus_one = sb("minus_one", [P, 2])
        var_eps = sb("var_eps", [P, 4])
        minus_mean = sb("minus_mean", [P, 4])
        rstd = sb("rstd", [P, 4])
        shift = sb("shift", [P, 4])

        xt_hi = sb("xt_hi", [P, DC, S], F32R, stage01)
        xt_lo = sb("xt_lo", [P, DC, S], F32R, stage01)
        affine = sb("affine", [P, 512], F32, stage01)
        tok = sb("tok", [P, SLOTS, D], F32, stage01)
        rowmax4 = sb("rowmax4", [P, 4], F32, stage01)
        rowmax = sb("rowmax", [P, 1], F32, stage01)
        bias = sb("bias", [P, 2], F32, stage01)
        sums4 = sb("sums4", [P, 2, 4], F32, stage01)
        rowsum = sb("rowsum", [P, 1], F32, stage01)
        rinv = sb("rinv", [P, 2], F32, stage01)

        setup = ExitStack()
        raw = [sb(f"raw{i}", [P, DC, D], F32, setup) for i in range(4)]
        raw_hi = [sb(f"raw_hi{i}", [P, DC, D], F32R, setup) for i in range(4)]
        raw_lo = [sb(f"raw_lo{i}", [P, DC, D], F32R, setup) for i in range(4)]
        setup.close()

        v_hi = sb("v_hi", [P, TILES, D], F32R, stage01)
        v_lo = sb("v_lo", [P, TILES, D], F32R, stage01)
        g_hi = sb("g_hi", [P, DC, GROUP * P], F32R, stage01)
        g_lo = sb("g_lo", [P, DC, GROUP * P], F32R, stage01)
        probs = sb("probs", [P, S], F32, stage01)
        pt_hi = sb("pt_hi", [P, 2, GROUP * P], F32R, stage01)
        pt_lo = sb("pt_lo", [P, 2, GROUP * P], F32R, stage01)
        stage01.close()

        TURN0 = 4
        ATTN = 6
        XBANK = 7

        consts_memset = sem("consts_memset")
        consts_ready = sem("consts_ready")
        small_consts_ready = sem("small_consts_ready")
        affine_loaded = sem("affine_loaded")
        PARTS = (slice(0, 1), slice(1, DC))
        weights_loaded = [[sem(f"weights_loaded{i}_{part}") for part in range(2)] for i in range(4)]
        weights_hi = sem("weights_hi")
        weights_split = sem("weights_split")
        fold_done = sem("fold_done")
        fold_hi = sem("fold_hi")
        fold_split = sem("fold_split")

        x_loaded = [sem(f"x_loaded{i}") for i in range(2)]
        x_normed = sem("x_normed")
        x_turned = sem("x_turned")
        affine_ready = sem("affine_ready")
        xt_hi_ready = sem("xt_hi_ready")
        xt_ready = sem("xt_ready")
        g_projected = sem("g_projected")
        g_hi_ready = sem("g_hi_ready")
        g_ready = sem("g_ready")
        v_projected = sem("v_projected")
        v_hi_ready = sem("v_hi_ready")
        v_ready = sem("v_ready")
        scores_ready = sem("scores_ready")
        bias_ready = sem("bias_ready")
        probs_ready = sem("probs_ready")
        probs_turned = sem("probs_turned")
        pt_hi_ready = sem("pt_hi_ready")
        pt_ready = sem("pt_ready")
        pv_done = sem("pv_done")
        res_loaded = [sem(f"res_loaded{i}") for i in range(SLOTS)]
        res_doubled = sem("res_doubled")
        attn_read = sem("attn_read")
        x1_ready = sem("x1_ready")
        x1_stored = [sem(f"x1_stored{i}") for i in range(SLOTS)]
        out_ready = sem("out_ready")
        out_stored = [sem(f"out_stored{i}") for i in range(SLOTS)]
        x_variance = sem("x_variance")
        x_rstd = sem("x_rstd")
        x_shift = sem("x_shift")
        variance_ready = sem("variance_ready")
        rstd_ready = sem("rstd_ready")
        shift_ready = sem("shift_ready")
        own = sem("own")

        PAIRS = TILES // 2
        FIRST_PAIRS = 3
        PEELED = 2
        XUNITS = 4

        def turn_bank(n):
            return TURN0 + n % 2

        TURNS = []
        for t in range(TILES):
            if t < GROUP:
                TURNS.append(("v", t))
            if t % GROUP == GROUP - 1 and t + 1 < TILES:
                TURNS += [("v", t + 1 + j) for j in range(GROUP)]
            TURNS += [("p", t, c) for c in range(chunks(t))]

        def turn_use(t, c):
            return TURNS.index(("p", t, c))

        def v_use(tile):
            return TURNS.index(("v", tile))

        NG = B * S // (GROUP * P)
        stage2 = ExitStack()
        whole.enter_context(stage2)
        x1_in = sb("x1_in", [P, 2, GROUP, D], F32, stage2)
        x1t_hi = sb("x1t_hi", [P, DC, GROUP * P], F32R, stage2)
        x1t_lo = sb("x1t_lo", [P, DC, GROUP * P], F32R, stage2)
        h1_hi = sb("h1_hi", [P, DC, GROUP * P], F32R, stage2)
        h1_lo = sb("h1_lo", [P, DC, GROUP * P], F32R, stage2)
        wr_s = sb("wr_s", [P, DC, P], F32R, stage2)
        gates_s = sb("gates_s", [P, GROUP, P], F32R, stage2)
        h2_hi = sb("h2_hi", [P, 2, D], F32R, stage2)
        h2_lo = sb("h2_lo", [P, 2, D], F32R, stage2)
        wr_raw = sb("wr_raw", [P, DC, E], F32, stage2)
        taken = 2 * GROUP * D + 4 * DC * GROUP * P + DC * P + GROUP * P + 4 * D + DC * E
        sb("not_yet_free", [P, 2 * DC * S - taken + (1 + SLOTS) * D + 64], F32, stage2)
        act_f = sb("act_f", [P, 2, D], F32, stage2)
        logits_t = sb("logits_t", [P, GROUP * P], F32, stage2)
        fold_rows = sb("fold_rows", [P, P], F32, stage2)
        expert_f = sb("expert_f", [P, GROUP, E], F32, stage2)
        euler = sb("euler", [P, GROUP, E], F32, stage2)
        logits = sb("logits", [P, GROUP, E], F32, stage2)
        lmax = sb("lmax", [P, GROUP], F32, stage2)
        shifted = sb("shifted", [P, GROUP, E], F32, stage2)
        expo = sb("expo", [P, GROUP, E], F32, stage2)
        esum = sb("esum", [P, GROUP], F32, stage2)
        erec = sb("erec", [P, GROUP], F32, stage2)
        route = sb("route", [P, GROUP, E], F32, stage2)
        best = sb("best", [P, GROUP, 8], F32, stage2)
        best_at = sb("best_at", [P, GROUP, 8], U32, stage2)
        best_at_f = sb("best_at_f", [P, GROUP, 8], F32, stage2)
        chosen = sb("chosen", [P, TOP_K, GROUP, E], F32, stage2)
        picked = sb("picked", [P, GROUP, E], F32, stage2)
        kept = sb("kept", [P, GROUP, E], F32, stage2)
        ksum = sb("ksum", [P, GROUP], F32, stage2)
        krec = sb("krec", [P, GROUP], F32, stage2)
        gate_f = sb("gate_f", [P, GROUP, E], F32, stage2)
        w2_sb = sb("w2_sb", [P, DC, D], F32, stage2)
        acc_sb = sb("acc_sb", [P, D], F32, stage2)
        acc_t = sb("acc_t", [P, DC, P], F32, stage2)
        rows = sb("rows", [E, D], F32, stage2)
        rows_out = sb("rows_out", [E, D], F32, stage2)
        rstats = sb("rstats", [E, 6], F32, stage2)
        rmeanvar = sb("rmeanvar", [E, 2], F32, stage2)
        rvar_eps = sb("rvar_eps", [E, 1], F32, stage2)
        rrstd = sb("rrstd", [E, 1], F32, stage2)

        LOGIT = 4
        LOGIT_T = 5
        ACC = 7
        FINAL = 6

        fold_memset = sem("fold_memset")
        fold_ready = sem("fold_ready")
        euler_ready = sem("euler_ready")
        iota_ready = sem("iota_ready")
        zeros_ready = sem("zeros_ready")
        w13_loaded = [sem(f"w13_loaded{i}") for i in range(2)]
        w2_loaded = sem("w2_loaded")
        wr_loaded = sem("wr_loaded")
        w13_hi = sem("w13_hi")
        w13_split = sem("w13_split")
        wr_hi = sem("wr_hi")
        wr_split = sem("wr_split")
        x1_loaded = [sem(f"x1_loaded{i}") for i in range(2)]
        x1_turned = sem("x1_turned")
        x1t_hi_ready = sem("x1t_hi_ready")
        x1t_ready = sem("x1t_ready")
        h1_product = sem("h1_product")
        h1_hi_ready = sem("h1_hi_ready")
        h1_ready = sem("h1_ready")
        h2_product = sem("h2_product")
        h2_hi_ready = sem("h2_hi_ready")
        h2_ready = sem("h2_ready")
        logits_product = sem("logits_product")
        logits_copied = sem("logits_copied")
        logits_turned = sem("logits_turned")
        logits_shifted = sem("logits_shifted")
        exp_ready = sem("exp_ready")
        gates_ready = sem("gates_ready")
        gated = sem("gated")
        rown = sem("rown")
        acc_done = sem("acc_done")
        acc_copied = sem("acc_copied")
        acc_turned = sem("acc_turned")
        acc_t_ready = sem("acc_t_ready")
        rows_product = sem("rows_product")
        rows_loaded = sem("rows_loaded")
        rows_variance = sem("rows_variance")
        rows_rstd = sem("rows_rstd")
        rows_ready = sem("rows_ready")
        rows_stored = sem("rows_stored")

        def fold_bank(n):
            return n if n < 7 else 3

        def h2_bank(n):
            return (n + 2) % 4

        def split_product(pe, bank, ws, w_lo, ms, m_lo_, first, last, n=512):
            o = psum[:, bank, 0:n]
            pe.matmul(o, ws, ms, start=first, stop=False, skip_group_check=True)
            pe.matmul(o, w_lo, ms, start=False, stop=False, skip_group_check=True)
            return pe.matmul(o, ws, m_lo_, start=False, stop=last, skip_group_check=True)

        block = whole.enter_context(nc.Block())

        start_at_one = [*out_stored, out_ready, shift_ready, xt_ready, affine_ready, probs_turned, pv_done, probs_ready, pt_ready,
                        attn_read, h2_ready, h1_hi_ready, h2_hi_ready, logits_copied]

        @block.sync
        def _(sp):
            for s in start_at_one:
                sp.sem_inc(s, 1)
            weights = [w.rearrange("(c p) n -> p c n", p=P) for w in (wq_t, wk_t, wv_t, wo)]
            for pair in range(2):
                for part, c in enumerate(PARTS):
                    for i in (2 * pair, 2 * pair + 1):
                        sp.dma_start(raw[i][:, c, :], weights[i][:, c, :]).then_inc(weights_loaded[i][part], DMA)
                if pair == 0:
                    sp.dma_start(gamma_sb[:], gamma).then_inc(affine_loaded, DMA)
                    sp.dma_start(beta_sb[:], beta).then_inc(affine_loaded, DMA)

            def store_x1(b, t):
                sp.wait_ge(x1_ready, b * TILES + t + 1)
                sp.dma_start(x1_scratch[bass.ds(b * S + t * P, P), :], tok[:, t % SLOTS, :]).then_inc(x1_stored[t % SLOTS], DMA)

            def store_out(b, t):
                sp.wait_ge(out_ready, 1 + b * TILES + t + 1)
                sp.dma_start(out[bass.ds(b * S + t * P, P), :], tok[:, t % SLOTS, :]).then_inc(out_stored[t % SLOTS], DMA)

            def tile(b, t, before=True):
                slot = t % SLOTS
                sp.wait_ge(out_stored[slot], 1 + (b * USES + t // SLOTS) * DMA)
                sp.dma_start(tok[:, slot, :], x[bass.ds(b * S + t * P, P), :]).then_inc(res_loaded[slot], DMA)
                if t >= 2:
                    store_x1(b, t - 2)
                elif before:
                    store_x1(b - 1, TILES + t - 2)
                if t >= 3:
                    store_out(b, t - 3)
                elif before:
                    store_out(b - 1, TILES + t - 3)

            for t in range(3):
                tile(0, t, before=False)
            with sp.Fori(0, B - 1) as b:
                for t in range(3, TILES):
                    tile(b, t)
                for t in range(3):
                    tile(b + 1, t)
            for t in range(3, TILES):
                tile(B - 1, t)
            for t in range(TILES - 2, TILES):
                store_x1(B - 1, t)
            for t in range(TILES - 3, TILES - 1):
                store_out(B - 1, t)

            for i in range(SLOTS):
                sp.wait_ge(x1_stored[i], B * USES * DMA)
            sp.wait_ge(pv_done, 1 + B * CHUNKS)
            sp.dma_start(w2_sb[:], w2_t.rearrange("(c p) n -> p c n", p=P)).then_inc(w2_loaded, DMA)
            sp.dma_start(rows[:], x1_scratch[0:E, :]).then_inc(rows_loaded, DMA)
            with sp.Fori(1, NG // 2) as h:
                for s in range(2):
                    sp.wait_ge(x1_turned, (2 * h - 1 + s) * DC)
                    sp.dma_start(x1_in[:, s], x1_scratch[bass.ds((2 * h + s) * 512, 512), :].rearrange("(t p) d -> p t d", p=P)).then_inc(x1_loaded[s], DMA)
            store_out(B - 1, TILES - 1)
            sp.wait_ge(rows_ready, 1)
            for i in range(SLOTS):
                sp.wait_ge(out_stored[i], 1 + B * USES * DMA)
            sp.dma_start(out[0:E, :], rows_out[:]).then_inc(rows_stored, DMA)
            sp.wait_ge(rows_stored, DMA)

        @block.gpsimd
        def _(pool):
            pool.memset(ident[:], 0.0).then_inc(consts_memset, 1)
            pool.memset(ident_bf[:], 0.0).then_inc(consts_memset, 1)
            pool.memset(mask_bf[:], 0.0).then_inc(consts_memset, 1)
            pool.wait_ge(consts_memset, 3)
            for m in (ident, ident_bf):
                pool.affine_select(out=m[:], in_=m[:], compare_op=ALU.not_equal, fill=1.0, base=0,
                                   pattern=[[-1, P]], channel_multiplier=1).then_inc(consts_ready, 1)
            pool.affine_select(out=mask_bf[:], in_=mask_bf[:], compare_op=ALU.is_ge, fill=MASKED, base=0,
                               pattern=[[-1, P]], channel_multiplier=1).then_inc(consts_ready, 1)

            pool.memset(minus_half[:], -0.5).then_inc(small_consts_ready, 1)
            pool.memset(minus_one[:], -1.0).then_inc(small_consts_ready, 1)
            pool.memset(eps[:], EPS).then_inc(small_consts_ready, 1)
            pool.wait_ge(small_consts_ready, 3)

            def scale_and_shift(a, z, rooted, roots_before, done):
                o = slice(0, z - a)
                pool.tensor_tensor(var_eps[:, a:z], meanvar[:, a:z, 1], eps[:, o], ALU.add).then_inc(rooted, 1)
                pool.tensor_tensor(minus_mean[:, a:z], meanvar[:, a:z, 0], minus_one[:, o], ALU.mult).then_inc(rooted, 1)
                pool.wait_ge(rooted, roots_before + 2)
                pool.tensor_tensor(rstd[:, a:z], var_eps[:, a:z], minus_half[:, o], ALU.pow).then_inc(rooted, 1)
                pool.wait_ge(rooted, roots_before + 3)
                pool.tensor_tensor(shift[:, a:z], minus_mean[:, a:z], rstd[:, a:z], ALU.mult).then_inc(done, 1)

            def norm_x(b, pair):
                n = b * PAIRS + pair
                pool.wait_ge(x_variance, n + 1)
                scale_and_shift(2, 4, x_rstd, n * 3, x_shift)

            def norm_behind(b, t, a=0, z=2):
                n = b * TILES + t
                pool.wait_ge(variance_ready, n + 1)
                if z == 2:
                    pool.wait_ge(out_ready, 1 + n - 1)
                scale_and_shift(a, z, rstd_ready, n * 3, shift_ready)

            def tile(b, t, last=False, before=True):
                g, k = t // GROUP, t % GROUP
                pool.wait_ge(res_loaded[t % SLOTS], (b * USES + t // SLOTS + 1) * DMA)
                y = tok[:, t % SLOTS, :]
                pool.tensor_tensor(y, y, y, ALU.add).then_inc(res_doubled, 1)
                if k == 3 and g + 2 < GROUPS:
                    norm_x(b, 2 * (g + 2))
                if k == 3 and g + 2 == GROUPS and not last:
                    norm_x(b + 1, 0)
                if t:
                    norm_behind(b, t - 1, z=2 if before or t > 1 else 1)
                elif before:
                    norm_behind(b - 1, TILES - 1)
                if t == TILES - 1 and not last:
                    norm_x(b + 1, 2)
                if k == 0 and g + 1 < GROUPS:
                    norm_x(b, 2 * (g + 1) + 1)
                if t == TILES - 2 and not last:
                    norm_x(b + 1, 1)

            def batch(b, last):
                for t in range(PEELED, TILES):
                    tile(b, t, last)
                if not last:
                    for t in range(PEELED):
                        tile(b + 1, t)

            for pair in range(FIRST_PAIRS):
                norm_x(0, pair)
            for t in range(PEELED):
                tile(0, t, before=False)
            with pool.Fori(0, B - 1) as b:
                batch(b, False)
            batch(B - 1, True)

            pool.wait_ge(scores_ready, B * CHUNKS)
            for buffer in (wr_s, gates_s, h2_hi, h2_lo):
                pool.memset(buffer[:].bitcast(F32), 0.0).then_inc(zeros_ready, 1)
            pool.wait_ge(pv_done, 1 + B * CHUNKS)
            pool.memset(fold_rows[:], 0.0).then_inc(fold_memset, 1)
            pool.wait_ge(fold_memset, 1)
            pool.affine_select(out=fold_rows[:], in_=fold_rows[:], compare_op=ALU.not_equal, fill=1.0, base=0,
                               pattern=[[-1, P]], channel_multiplier=1).then_inc(fold_memset, 1)
            pool.wait_ge(fold_memset, 2)
            pool.affine_select(out=fold_rows[:], in_=fold_rows[:], compare_op=ALU.not_equal, fill=1.0, base=-E,
                               pattern=[[-1, P]], channel_multiplier=1).then_inc(fold_ready, 1)
            pool.iota(expert_f[:], pattern=[[0, GROUP], [1, E]], base=0, channel_multiplier=0,
                      allow_small_or_imprecise_dtypes=True).then_inc(iota_ready, 1)
            pool.memset(euler[:], 2.718281828459045).then_inc(euler_ready, 1)
            pool.wait_ge(euler_ready, 1)
            norm_behind(B - 1, TILES - 1)

            def exp(i):
                pool.wait_ge(logits_shifted, i + 1)
                pool.tensor_tensor(expo[:], euler[:], shifted[:], ALU.pow).then_inc(exp_ready, 1)

            with pool.Fori(0, NG - 1) as i:
                exp(i)
            norm_behind(B, 0, 1, 2)
            exp(NG - 1)
            pool.wait_ge(rows_variance, 1)
            pool.tensor_tensor(rrstd[:], rvar_eps[:], minus_half[0:E, 0:1], ALU.pow).then_inc(rows_rstd, 1)

        @block.scalar
        def _(act):
            def weights_to_hi(pair, chunks_=range(DC)):
                for c in chunks_:
                    for i in (2 * pair, 2 * pair + 1):
                        act.wait_ge(weights_loaded[i][min(c, 1)], DMA)
                        act.activation(raw_hi[i][:, c, :], raw[i][:, c, :], ACT.Copy).then_inc(weights_hi, 1)

            def fold_to_hi(pair):
                for n in range(pair * DC, (pair + 1) * DC):
                    act.wait_ge(fold_done, n + 1)
                    act.activation((m_hi, wvo_hi)[pair][:, n % DC, :], psum[:, fold_bank(n), :], ACT.Copy).then_inc(fold_hi, 1)

            def load_x(b, pair):
                for slot in range(2):
                    act.dma_start(xin[:, slot, :], x[bass.ds(b * S + (2 * pair + slot) * P, P), :]).then_inc(x_loaded[slot], DMA)

            def turn_x(b, g, u, more=True):
                n = g * XUNITS + u
                act.wait_ge(xt_ready, 1 + b * (GROUPS * XUNITS) + n)
                act.wait_ge(x_turned, b * (GROUPS * XUNITS) + n + 1)
                for k in range(2):
                    c = 2 * (u % 2) + k
                    last = act.activation(affine[:, 256 * k:256 * (k + 1)], psum[:, XBANK, 256 * k:256 * (k + 1)],
                                          ACT.Identity, bias=beta_sb[:, c:c + 1], scale=gamma_sb[:, c:c + 1])
                last.then_inc(affine_ready, 1)
                if u % 2 == 1 and more:
                    if n // 2 + 1 < TILES // 2:
                        load_x(b, n // 2 + 1)
                    else:
                        load_x(b + 1, 0)

            def project_g(b, g):
                for j in range(DC):
                    act.wait_ge(g_projected, b * (GROUPS * DC) + g * DC + j + 1)
                    act.activation(g_hi[:, j, :], psum[:, j, :], ACT.Copy).then_inc(g_hi_ready, 1)

            def normalise(slot, o, y):
                return act.activation(o, y, ACT.Identity, bias=shift[:, slot:slot + 1], scale=rstd[:, slot:slot + 1])

            def norm_x(b, pair):
                act.wait_ge(x_shift, b * PAIRS + pair + 1)
                normalise(2, xin[:, 0, :], xin[:, 0, :])
                normalise(3, xin[:, 1, :], xin[:, 1, :]).then_inc(x_normed, 1)

            def norm_behind(b, t, slots=(0, 1)):
                act.wait_ge(shift_ready, 1 + b * TILES + t + 1)
                if 0 in slots:
                    y = tok[:, t % SLOTS, :]
                    normalise(0, y, y).then_inc(x1_ready, 1)
                if 1 in slots:
                    slot = (t - 1) % SLOTS
                    act.wait_ge(x1_stored[slot], (b * USES + (t - 1) // SLOTS + 1) * DMA)
                    y = tok[:, slot, :]
                    normalise(1, y, y).then_inc(out_ready, 1)

            def project_v(b, tile):
                act.wait_ge(v_projected, b * TILES + tile + 1)
                act.activation(v_hi[:, tile, :], psum[:, turn_bank(v_use(tile)), :], ACT.Copy).then_inc(v_hi_ready, 1)

            def exp(b, t, c):
                if c == 0:
                    act.wait_ge(bias_ready, b * TILES + t + 1)
                w, at = width(t, c), key_start(t, c)
                if t:
                    overlap = [u for u in range(chunks(t - 1)) if key_start(t - 1, u) < at + w]
                    act.wait_ge(probs_turned, 1 + b * CHUNKS + BEFORE[t - 1] + overlap[-1] + 1)
                act.activation(probs[:, at:at + w], psum[:, c, 0:w], ACT.Exp, bias=bias[:, t % 2:t % 2 + 1],
                               scale=SCALE, accum_out=sums4[:, t % 2, c:c + 1]).then_inc(probs_ready, 1)

            def exp_first(b):
                act.wait_ge(bias_ready, (b + 1) * TILES + 1)
                act.wait_ge(probs_turned, 1 + b * CHUNKS + BEFORE[TILES - 1] + 1)
                w = width(0, 0)
                act.activation(probs[:, 0:w], psum[:, 0, 0:w], ACT.Exp, bias=bias[:, 0:1],
                               scale=SCALE, accum_out=sums4[:, 0, 0:1]).then_inc(probs_ready, 1)

            def turn_probs(b, t, c):
                n = BEFORE[t] + c
                act.wait_ge(probs_turned, 1 + b * CHUNKS + n + 1)
                act.wait_ge(pv_done, 1 + b * CHUNKS + max(n - 1, 0))
                w = width(t, c)
                act.activation(pt_hi[:, n % 2, 0:w], psum[:, turn_bank(turn_use(t, c)), 0:w], ACT.Copy).then_inc(pt_hi_ready, 1)

            def load_w13(j):
                for n in (j, j + 1):
                    w = (w1_t, w3_t)[n // DC]
                    act.dma_start(xin[:, n % 2, :], w[n % DC * P:(n % DC + 1) * P, :]).then_inc(w13_loaded[n % 2], DMA)

            def split_w13(j):
                for n in (j, j + 1):
                    act.wait_ge(w13_loaded[n % 2], (n // 2 + 1) * DMA)
                    act.activation((w1_hi, w3_hi)[n // DC][:, n % DC, :], xin[:, n % 2, :], ACT.Copy).then_inc(w13_hi, 1)

            def tile(b, t, last=False, before=True):
                g, k = t // GROUP, t % GROUP
                more = g + 1 < GROUPS
                n_next = chunks(t + 1) if t + 1 < TILES else 0
                turn_probs(b, t, 0)
                if more and k == 0:
                    turn_x(b, g + 1, 0)
                if chunks(t) > 1:
                    turn_probs(b, t, 1)
                if more and k == 0:
                    turn_x(b, g + 1, 1)
                if more and k == 2:
                    turn_x(b, g + 1, 2)
                if t == TILES - 2 and not last:
                    turn_x(b + 1, 0, 0)
                if t == TILES - 1 and not last:
                    turn_x(b + 1, 0, 2)
                if more and k == 1:
                    norm_x(b, 2 * (g + 1) + 1)
                for c in range(max(chunks(t), n_next)):
                    if c >= 2 and c < chunks(t):
                        turn_probs(b, t, c)
                    if more and k == 2 and c == chunks(t) - 1:
                        turn_x(b, g + 1, 3, more=not (last and g + 2 == GROUPS))
                    if c < n_next:
                        exp(b, t + 1, c)
                    if t == 0 and before:
                        norm_behind(b - 1, TILES - 2)
                    if c == 0 and t + 1 < GROUP:
                        project_v(b, t + 1)
                    if c == 1 and t == TILES - 2 and not last:
                        turn_x(b + 1, 0, 1)
                    if c == 1 and t == TILES - 1 and not last:
                        turn_x(b + 1, 0, 3)
                    if c == 2 and t == TILES - 1 and not last:
                        project_g(b + 1, 0)
                if k == 3 and g + 2 < GROUPS:
                    norm_x(b, 2 * (g + 2))
                if k == 3 and g + 2 == GROUPS and not last:
                    norm_x(b + 1, 0)
                if t and not (t == TILES - 1 and not last):
                    norm_behind(b, t - 1, (0, 1) if before or t > 1 else (0,))
                if t == TILES - 2 and not last:
                    norm_x(b + 1, 1)
                if more and k == 2:
                    project_v(b, GROUP * (g + 1))
                    project_g(b, g + 1)
                    for j in range(1, GROUP):
                        project_v(b, GROUP * (g + 1) + j)
                if t == TILES - 1 and not last:
                    exp_first(b)
                    norm_x(b + 1, 2)
                    project_v(b + 1, 0)
                if t == 0 and before:
                    norm_behind(b - 1, TILES - 1)
                from_tile = TILES - 1 - GROUP
                if last and from_tile <= t < TILES - 1:
                    split_w13(2 * (t - from_tile))
                if last and from_tile - 1 <= t < TILES - 2:
                    if t >= from_tile:
                        act.wait_ge(w13_split, 2 * (t - from_tile) + 2)
                    load_w13(2 * (t - from_tile) + 2)
                if last and t == TILES - 2:
                    act.wait_ge(scores_ready, B * CHUNKS)
                    for i in range(SLOTS):
                        act.wait_ge(x1_stored[i], 2 * GROUP // SLOTS * DMA)
                    for i in range(2):
                        act.dma_start(x1_in[:, i], x1_scratch[i * 512:(i + 1) * 512, :].rearrange("(t p) d -> p t d", p=P)).then_inc(x1_loaded[i], DMA)
                    act.dma_start(wr_raw[:], wr_t.rearrange("(c p) n -> p c n", p=P)).then_inc(wr_loaded, DMA)

            def batch(b, last):
                for t in range(PEELED, TILES):
                    tile(b, t, last)
                if not last:
                    for t in range(PEELED):
                        tile(b + 1, t)
            load_x(0, 0)
            weights_to_hi(0, range(1))
            norm_x(0, 0)
            weights_to_hi(0, range(1, 2))
            act.wait_ge(affine_loaded, 2 * DMA)
            turn_x(0, 0, 0)
            weights_to_hi(0, range(2, 3))
            turn_x(0, 0, 1)
            weights_to_hi(0, range(3, DC))
            weights_to_hi(1, range(3))
            norm_x(0, 1)
            fold_to_hi(0)
            weights_to_hi(1, range(3, DC))
            turn_x(0, 0, 2)
            turn_x(0, 0, 3)
            fold_to_hi(1)
            project_g(0, 0)
            exp(0, 0, 0)
            norm_x(0, 2)
            project_v(0, 0)
            for t in range(PEELED):
                tile(0, t, before=False)
            with act.Fori(0, B - 1) as b:
                batch(b, False)
            batch(B - 1, True)

            def turn_x1(i, c):
                act.wait_ge(x1_turned, i * DC + c + 1)
                act.activation(x1t_hi[:, c, :], psum[:, c, :], ACT.Copy).then_inc(x1t_hi_ready, 1)

            def silu(bank, n, hi, done):
                act.activation(act_f[:, n % 2, :], psum[:, bank, :], ACT.Silu)
                act.activation(hi, psum[:, bank, :], ACT.Silu).then_inc(done, 1)

            def group(i, last):
                for n in range(DC):
                    act.wait_ge(h1_product, i * 4 + n + 1)
                    if n < 2:
                        act.wait_ge(h2_ready, 1 + i * 4)
                    else:
                        act.wait_ge(h1_ready, i * 4 + n - 1)
                    silu(n, n, h1_hi[:, n, :], h1_hi_ready)
                if not last:
                    turn_x1(i + 1, 0)
                    turn_x1(i + 1, 1)
                for n in range(GROUP):
                    if n == 3 and not last:
                        turn_x1(i + 1, 2)
                        turn_x1(i + 1, 3)
                    act.wait_ge(h2_product, i * 4 + n + 1)
                    if n < 2:
                        act.wait_ge(h1_ready, i * 4 + 3 + n)
                    else:
                        act.wait_ge(h2_ready, 1 + i * 4 + n - 1)
                        act.wait_ge(gated, i * 4 + n)
                    silu(h2_bank(n), n, h2_hi[:, n % 2, :], h2_hi_ready)

            for c in range(DC):
                turn_x1(0, c)
            norm_behind(B - 1, TILES - 1)
            with act.Fori(0, NG - 1) as i:
                group(i, False)
            norm_behind(B, 0, (1,))
            group(NG - 1, True)
            act.wait_ge(acc_done, 1)
            act.activation(acc_sb[:], psum[:, ACC, :], ACT.Copy).then_inc(acc_copied, 1)
            for c in range(DC):
                act.wait_ge(acc_turned, c + 1)
                act.activation(acc_t[:, c, :], psum[:, c, 0:P], ACT.Copy).then_inc(acc_t_ready, 1)

        @block.vector
        def _(dve):
            def carry_wait():
                dve.memset(unused[:], 0.0)

            def weights_to_lo(pair, chunks_=range(DC)):
                for c in chunks_:
                    for k in range(2):
                        i = 2 * pair + k
                        dve.wait_ge(weights_hi, pair * 2 * DC + 2 * c + k + 1)
                        dve.tensor_tensor(raw_lo[i][:, c, :], raw[i][:, c, :], raw_hi[i][:, c, :], ALU.subtract).then_inc(weights_split, 1)

            def fold_to_lo(pair):
                hi, lo = ((m_hi, m_lo), (wvo_hi, wvo_lo))[pair]
                for n in range(pair * DC, (pair + 1) * DC):
                    dve.wait_ge(fold_hi, n + 1)
                    dve.tensor_tensor(lo[:, n % DC, :], psum[:, fold_bank(n), :], hi[:, n % DC, :], ALU.subtract).then_inc(fold_split, 1)

            FIRST_OWN = FIRST_PAIRS + 1 + 8
            OWN = PAIRS + TILES + TILES * 3 + (TILES - GROUP)
            count, last_own = [0], [0]
            at_batch = [0]

            def mine(instruction):
                instruction.then_inc(own, 1)
                count[0] += 1
                dve.wait_ge(own, at_batch[0] * OWN + count[0])

            def statistics(rows_of, a, z, requested):
                for s in range(a, z):
                    done = dve.bn_stats(stats[:, s, :], rows_of(s))
                mine(done)
                carry_wait()
                for s in range(a, z):
                    done = dve.bn_aggr(meanvar[:, s, :], stats[:, s, :])
                done.then_inc(requested, 1)

            def norm_x(b, pair):
                for s in range(2):
                    dve.wait_ge(x_loaded[s], b * (TILES // 2 * DMA) + (pair + 1) * DMA)
                statistics(lambda s: xin[:, s - 2, :], 2, 4, x_variance)

            def split_x(b, g, u):
                at = (GROUP * g + 2 * (u // 2)) * P
                c = 2 * (u % 2)
                n = b * (GROUPS * XUNITS) + g * XUNITS + u + 1
                value = affine[:].rearrange("p (k n) -> p k n", k=2)
                dve.wait_ge(affine_ready, 1 + n)
                dve.tensor_copy(xt_hi[:, c:c + 2, at:at + 256], value).then_inc(xt_hi_ready, 1)
                dve.wait_ge(xt_hi_ready, n)
                dve.tensor_tensor(xt_lo[:, c:c + 2, at:at + 256], value, xt_hi[:, c:c + 2, at:at + 256],
                                  ALU.subtract).then_inc(xt_ready, 1)

            def split_g(b, g):
                for j in range(DC):
                    dve.wait_ge(g_hi_ready, b * (GROUPS * DC) + g * DC + j + 1)
                    dve.tensor_tensor(g_lo[:, j, :], psum[:, j, :], g_hi[:, j, :], ALU.subtract).then_inc(g_ready, 1)

            def split_v(b, tile):
                dve.wait_ge(v_hi_ready, b * TILES + tile + 1)
                dve.tensor_tensor(v_lo[:, tile, :], psum[:, turn_bank(v_use(tile)), :], v_hi[:, tile, :],
                                  ALU.subtract).then_inc(v_ready, 1)

            def split_probs(b, t, c):
                n, w = BEFORE[t] + c, width(t, c)
                dve.wait_ge(pt_hi_ready, b * CHUNKS + n + 1)
                dve.tensor_tensor(pt_lo[:, n % 2, 0:w], psum[:, turn_bank(turn_use(t, c)), 0:w],
                                  pt_hi[:, n % 2, 0:w], ALU.subtract).then_inc(pt_ready, 1)

            def chunk_max(b, t, c):
                dve.wait_ge(scores_ready, b * CHUNKS + BEFORE[t] + c + 1)
                return dve.tensor_reduce((rowmax if chunks(t) == 1 else rowmax4)[:, c:c + 1], psum[:, c, 0:width(t, c)], AX.X, ALU.max)

            def row_bias(b, t):
                mine(chunk_max(b, t, chunks(t) - 1))
                if chunks(t) > 1:
                    mine(dve.tensor_reduce(rowmax[:], rowmax4[:, 0:chunks(t)], AX.X, ALU.max))
                dve.tensor_scalar(bias[:, t % 2:t % 2 + 1], rowmax[:], -SCALE, None, ALU.mult).then_inc(bias_ready, 1)

            def row_sum(b, t):
                dve.wait_ge(probs_ready, 1 + b * CHUNKS + BEFORE[t + 1])
                mine(dve.tensor_reduce(rowsum[:], sums4[:, t % 2, 0:chunks(t)], AX.X, ALU.add))
                mine(dve.reciprocal(rinv[:, t % 2:t % 2 + 1], rowsum[:]))

            def residual(b, t):
                dve.wait_ge(pv_done, 1 + b * CHUNKS + BEFORE[t + 1])
                dve.wait_ge(res_doubled, b * TILES + t + 1)
                y = tok[:, t % SLOTS, :]
                dve.scalar_tensor_tensor(out=y, in0=psum[:, ATTN, :], scalar=rinv[:, t % 2:t % 2 + 1], in1=y,
                                         op0=ALU.mult, op1=ALU.add).then_inc(attn_read, 1)

            def norm_behind(b, t, a=0, z=2):
                if z == 2:
                    dve.wait_ge(shift_ready, 1 + b * TILES + t)
                    dve.wait_ge(x1_ready, b * TILES + t)
                if a == 0:
                    dve.wait_ge(attn_read, 1 + b * TILES + t + 1)
                statistics(lambda s: tok[:, (t - s) % SLOTS, :], a, z, variance_ready)

            def split_w13(j):
                for n in (j, j + 1):
                    dve.wait_ge(w13_hi, n + 1)
                    dve.tensor_tensor((w1_lo, w3_lo)[n // DC][:, n % DC, :], xin[:, n % 2, :], (w1_hi, w3_hi)[n // DC][:, n % DC, :],
                                      ALU.subtract).then_inc(w13_split, 1)

            def tile(b, t, last=False, before=True):
                g, k = t // GROUP, t % GROUP
                more = g + 1 < GROUPS
                if t:
                    residual(b, t - 1)
                if t + 1 < TILES:
                    for c in range(chunks(t + 1) - 1):
                        chunk_max(b, t + 1, c)
                split_probs(b, t, 0)
                if more and k == 0:
                    split_x(b, g + 1, 0)
                if t + 1 < TILES:
                    row_bias(b, t + 1)
                row_sum(b, t)
                if chunks(t) > 1:
                    split_probs(b, t, 1)
                if more and k == 0:
                    split_x(b, g + 1, 1)
                if more and k == 2:
                    split_x(b, g + 1, 2)
                if t == TILES - 2 and not last:
                    split_x(b + 1, 0, 0)
                if t == TILES - 1 and not last:
                    split_x(b + 1, 0, 2)
                if k == 3 and g + 2 < GROUPS:
                    norm_x(b, 2 * (g + 2))
                if k == 3 and g + 2 == GROUPS and not last:
                    norm_x(b + 1, 0)
                if t:
                    norm_behind(b, t - 1, z=2 if before or t > 1 else 1)
                elif before:
                    norm_behind(b - 1, TILES - 1)
                if t + 1 < GROUP:
                    split_v(b, t + 1)
                if t == TILES - 2 and not last:
                    split_x(b + 1, 0, 1)
                if t == TILES - 1 and not last:
                    split_x(b + 1, 0, 3)
                if chunks(t) > 2:
                    split_probs(b, t, 2)
                if t == TILES - 1 and not last:
                    split_g(b + 1, 0)
                if chunks(t) > 3:
                    split_probs(b, t, 3)
                if t == TILES - 1 and last:
                    split_wr()
                if more and k == 2:
                    split_x(b, g + 1, 3)
                    split_v(b, GROUP * (g + 1))
                    split_g(b, g + 1)
                    for j in range(1, GROUP):
                        split_v(b, GROUP * (g + 1) + j)
                if more and k == 0:
                    norm_x(b, 2 * (g + 1) + 1)
                if t == TILES - 2 and not last:
                    norm_x(b + 1, 1)
                from_tile = TILES - 1 - GROUP
                if last and from_tile <= t < TILES - 1:
                    split_w13(2 * (t - from_tile))
            def batch(b, last):
                at_batch[0] = b
                count[0] = FIRST_OWN
                for t in range(PEELED, TILES):
                    tile(b, t, last)
                if last:
                    residual(b, TILES - 1)
                    split_first_x1()
                    norm_behind(b, TILES - 1)
                    last_own[0] = count[0]
                else:
                    row_bias(b + 1, 0)
                    norm_x(b + 1, 2)
                    residual(b, TILES - 1)
                    split_v(b + 1, 0)
                    for t in range(PEELED):
                        tile(b + 1, t)
                    assert count[0] == FIRST_OWN + OWN

            def split_wr():
                dve.wait_ge(zeros_ready, 4)
                dve.wait_ge(wr_loaded, DMA)
                dve.tensor_copy(wr_s[:, :, 0:E], wr_raw[:]).then_inc(wr_hi, 1)
                dve.wait_ge(wr_hi, 1)
                dve.tensor_tensor(wr_s[:, :, E:2 * E], wr_raw[:], wr_s[:, :, 0:E], ALU.subtract).then_inc(wr_split, 1)

            def split_first_x1():
                for c in range(DC):
                    dve.wait_ge(x1t_hi_ready, c + 1)
                    dve.tensor_tensor(x1t_lo[:, c, :], psum[:, c, :], x1t_hi[:, c, :], ALU.subtract).then_inc(x1t_ready, 1)

            norm_x(0, 0)
            weights_to_lo(0, range(2))
            split_x(0, 0, 0)
            weights_to_lo(0, range(2, 3))
            split_x(0, 0, 1)
            weights_to_lo(0, range(3, DC))
            norm_x(0, 1)
            weights_to_lo(1, range(2))
            fold_to_lo(0)
            weights_to_lo(1, range(2, DC))
            split_x(0, 0, 2)
            split_x(0, 0, 3)
            fold_to_lo(1)
            norm_x(0, 2)
            split_g(0, 0)
            row_bias(0, 0)
            split_v(0, 0)
            for t in range(PEELED):
                tile(0, t, before=False)
            assert count[0] == FIRST_OWN
            with dve.Fori(0, B - 1) as b:
                batch(b, False)
            batch(B - 1, True)

            dve.wait_ge(iota_ready, 1)

            ROUTE = 15

            def group(i, last):
                count = [0]

                def mine(instruction):
                    instruction.then_inc(rown, 1)
                    count[0] += 1
                    dve.wait_ge(rown, i * ROUTE + count[0])

                def spread(a):
                    return a.unsqueeze(2).to_broadcast([P, GROUP, E])

                def split_x1(c):
                    dve.wait_ge(x1t_hi_ready, (i + 1) * DC + c + 1)
                    dve.tensor_tensor(x1t_lo[:, c, :], psum[:, c, :], x1t_hi[:, c, :], ALU.subtract).then_inc(x1t_ready, 1)

                def split_h2(n):
                    dve.wait_ge(h2_hi_ready, 1 + i * 4 + n + 1)
                    dve.tensor_tensor(h2_lo[:, n % 2, :], act_f[:, n % 2, :], h2_hi[:, n % 2, :], ALU.subtract).then_inc(h2_ready, 1)

                def split_h1(n):
                    dve.wait_ge(h1_hi_ready, 1 + i * 4 + n + 1)
                    dve.tensor_tensor(h1_lo[:, n, :], act_f[:, n % 2, :], h1_hi[:, n, :], ALU.subtract).then_inc(h1_ready, 1)

                dve.wait_ge(logits_product, i + 1)
                dve.tensor_copy(logits_t[:], psum[:, LOGIT, :]).then_inc(logits_copied, 1)
                split_h1(0)
                dve.wait_ge(logits_turned, i + 1)
                halves = psum[:, LOGIT_T, :].rearrange("p (t e) -> p t e", e=P)
                mine(dve.tensor_copy(logits[:], halves[:, :, 0:E]))
                mine(dve.tensor_tensor(logits[:], logits[:], halves[:, :, E:2 * E], ALU.add))
                mine(dve.tensor_reduce(lmax[:], logits[:], AX.X, ALU.max))
                dve.tensor_tensor(shifted[:], logits[:], spread(lmax[:]), ALU.subtract).then_inc(logits_shifted, 1)
                split_h1(1)
                split_h1(2)
                dve.wait_ge(exp_ready, i + 1)
                mine(dve.tensor_reduce(esum[:], expo[:], AX.X, ALU.add))
                mine(dve.reciprocal(erec[:], esum[:]))
                mine(dve.tensor_tensor(route[:], expo[:], spread(erec[:]), ALU.mult))
                carry_wait()
                for t in range(GROUP):
                    largest = dve.max(best[:, t, :], route[:, t, :])
                mine(largest)
                carry_wait()
                for t in range(GROUP):
                    at = dve.max_index(best_at[:, t, :], best[:, t, :], route[:, t, :])
                mine(at)
                split_h1(3)
                mine(dve.tensor_copy(best_at_f[:], best_at[:]))
                for k in range(TOP_K):
                    one_hot = dve.tensor_tensor(chosen[:, k], expert_f[:], best_at_f[:, :, k:k + 1].to_broadcast([P, GROUP, E]), ALU.is_equal)
                mine(one_hot)
                mine(dve.tensor_tensor(picked[:], chosen[:, 0], chosen[:, 1], ALU.add))
                mine(dve.tensor_tensor(kept[:], route[:], picked[:], ALU.mult))
                mine(dve.tensor_reduce(ksum[:], kept[:], AX.X, ALU.add))
                mine(dve.reciprocal(krec[:], ksum[:]))
                dve.wait_ge(gated, i * 4 + 1)
                mine(dve.tensor_tensor(gate_f[:], kept[:], spread(krec[:]), ALU.mult))
                assert count[0] == ROUTE, count[0]
                dve.tensor_copy(gates_s[:, :, 0:E], gate_f[:]).then_inc(gates_ready, 1)
                dve.wait_ge(gates_ready, 2 * i + 1)
                dve.tensor_tensor(gates_s[:, :, E:2 * E], gate_f[:], gates_s[:, :, 0:E], ALU.subtract).then_inc(gates_ready, 1)
                if not last:
                    split_x1(0)
                    split_x1(1)
                for n in range(GROUP):
                    if n == 3 and not last:
                        split_x1(2)
                        split_x1(3)
                    split_h2(n)

            with dve.Fori(0, NG - 1) as i:
                group(i, False)
            at_batch[0], count[0] = B - 1, last_own[0]
            norm_behind(B, 0, 1, 2)
            group(NG - 1, True)

            dve.wait_ge(rows_loaded, DMA)
            dve.wait_ge(rows_product, 1)
            done = NG * ROUTE
            dve.tensor_tensor(rows[:], rows[:], psum[0:E, FINAL, :], ALU.add).then_inc(rown, 1)
            dve.wait_ge(rown, done + 1)
            dve.bn_stats(rstats[:], rows[:]).then_inc(rown, 1)
            dve.wait_ge(rown, done + 2)
            dve.bn_aggr(rmeanvar[:], rstats[:]).then_inc(rown, 1)
            dve.wait_ge(rown, done + 3)
            dve.tensor_scalar(rvar_eps[:], rmeanvar[:, 1:2], EPS, None, ALU.add).then_inc(rows_variance, 1)
            dve.wait_ge(rows_rstd, 1)
            dve.tensor_scalar(rows_out[:], rows[:], rmeanvar[:, 0:1], rrstd[:], ALU.subtract, ALU.mult).then_inc(rows_ready, 1)

        @block.tensor
        def _(pe):
            def fold_weights(pair, chunks_):
                a, w = 2 * pair, 2 * pair + 1
                for c in chunks_:
                    pe.wait_ge(weights_split, pair * 2 * DC + 2 * c + 2)
                    for n in range(DC):
                        if pair == 1 and c == 0 and n == DC - 1:
                            pe.wait_ge(fold_split, DC)
                        rows_at = slice(n * P, (n + 1) * P)
                        last = split_product(pe, fold_bank(pair * DC + n), raw_hi[a][:, c, rows_at], raw_lo[a][:, c, rows_at],
                                             raw_hi[w][:, c, :], raw_lo[w][:, c, :], c == 0, c == DC - 1)
                        if c == DC - 1:
                            last.then_inc(fold_done, 1)

            def turn_x(b, g, u):
                n = g * XUNITS + u
                if u % 2 == 0:
                    pe.wait_ge(x_normed, b * (TILES // 2) + n // 2 + 1)
                pe.wait_ge(affine_ready, 1 + b * (GROUPS * XUNITS) + n)
                for k in range(2):
                    c = 2 * (u % 2) + k
                    for tile in range(2):
                        at = 256 * k + P * tile
                        last = pe.transpose(psum[:, XBANK, at:at + P], xin[:, tile, c * P:(c + 1) * P], ident[:])
                last.then_inc(x_turned, 1)

            def project_g(b, g, first=False):
                pe.wait_ge(probs_ready, 1 + b * CHUNKS + BEFORE[GROUP * g])
                at = slice(GROUP * g * P, GROUP * (g + 1) * P)
                for half in range(2):
                    pe.wait_ge(xt_ready, 1 + b * (GROUPS * XUNITS) + g * XUNITS + 3 + half)
                    for j in range(DC):
                        if first and half == 0 and j in (0, DC - 1):
                            pe.wait_ge(fold_split, (1 if j == 0 else 2) * DC)
                        cols = slice(j * P, (j + 1) * P)
                        for c in (2 * half, 2 * half + 1):
                            last = split_product(pe, j, m_hi[:, c, cols], m_lo[:, c, cols],
                                                 xt_hi[:, c, at], xt_lo[:, c, at], c == 0, c == DC - 1)
                        if half == 1:
                            last.then_inc(g_projected, 1)

            def project_v(b, tile):
                n = v_use(tile)
                free_turn_bank(b, n)
                at = slice(tile * P, (tile + 1) * P)
                for c in range(DC):
                    last = split_product(pe, turn_bank(n), xt_hi[:, c, at], xt_lo[:, c, at],
                                         wvo_hi[:, c, :], wvo_lo[:, c, :], c == 0, c == DC - 1)
                last.then_inc(v_projected, 1)

            def free_turn_bank(b, n):
                if n < 2:
                    pe.wait_ge(pt_ready, 1 + b * CHUNKS)
                elif TURNS[n - 2][0] == "v":
                    pe.wait_ge(v_ready, b * TILES + TURNS[n - 2][1] + 1)
                else:
                    _, t, c = TURNS[n - 2]
                    pe.wait_ge(pt_ready, 1 + b * CHUNKS + BEFORE[t] + c + 1)

            def score(b, t, c):
                pe.wait_ge(probs_ready, 1 + b * CHUNKS + (min(BEFORE[t - 1] + c + 1, BEFORE[t]) if t else 0))
                w = width(t, c)
                q = slice(t % GROUP * P, (t % GROUP + 1) * P)
                keys = slice(key_start(t, c), key_start(t, c) + w)
                for k in range(DC):
                    if c == 0 and t % GROUP == 0:
                        pe.wait_ge(g_ready, b * (GROUPS * DC) + (t // GROUP) * DC + k + 1)
                    last = split_product(pe, c, g_hi[:, k, q], g_lo[:, k, q], xt_hi[:, k, keys], xt_lo[:, k, keys],
                                         k == 0, k == DC - 1, w)
                    if k == 0 and c == chunks(t) - 1:
                        pe.matmul(psum[:, c, w - P:w], ident_bf[:], mask_bf[:], start=False, stop=False, skip_group_check=True)
                last.then_inc(scores_ready, 1)

            def turn_probs(b, t, c):
                n = turn_use(t, c)
                pe.wait_ge(probs_ready, 1 + b * CHUNKS + BEFORE[t] + c + 1)
                free_turn_bank(b, n)
                for k in range(width(t, c) // P):
                    last = pe.transpose(psum[:, turn_bank(n), k * P:(k + 1) * P],
                                        probs[:, key_start(t, c) + k * P:key_start(t, c) + (k + 1) * P], ident[:])
                last.then_inc(probs_turned, 1)

            def attend(b, t, c):
                n = BEFORE[t] + c
                if c == 0:
                    pe.wait_ge(attn_read, 1 + b * TILES + t)
                    if t < GROUP or t % GROUP == 0:
                        pe.wait_ge(v_ready, b * TILES + (t + 1 if t < GROUP else t + GROUP))
                pe.wait_ge(pt_ready, 1 + b * CHUNKS + n + 1)
                blocks = width(t, c) // P
                for k in range(blocks):
                    at = slice(k * P, (k + 1) * P)
                    key = key_start(t, c) // P + k
                    last = split_product(pe, ATTN, pt_hi[:, n % 2, at], pt_lo[:, n % 2, at], v_hi[:, key, :], v_lo[:, key, :],
                                         key == 0, c == chunks(t) - 1 and k == blocks - 1)
                last.then_inc(pv_done, 1)

            def tile(b, t, last=False, before=True):
                g, k = t // GROUP, t % GROUP
                more = g + 1 < GROUPS
                if t + 1 < TILES:
                    for c in range(chunks(t + 1) - 1):
                        score(b, t + 1, c)
                turn_probs(b, t, 0)
                if more and k == 0:
                    turn_x(b, g + 1, 0)
                if t + 1 < TILES:
                    score(b, t + 1, chunks(t + 1) - 1)
                if more and k == 0:
                    turn_x(b, g + 1, 1)
                if more and k == 2:
                    turn_x(b, g + 1, 2)
                if t == TILES - 2 and not last:
                    turn_x(b + 1, 0, 0)
                if t == TILES - 1 and not last:
                    turn_x(b + 1, 0, 2)
                if t + 1 < GROUP:
                    project_v(b, t + 1)
                for c in range(chunks(t)):
                    if c + 1 < chunks(t):
                        turn_probs(b, t, c + 1)
                    if more and k == 2 and c == chunks(t) - 1:
                        turn_x(b, g + 1, 3)
                    if c == 1 and t == TILES - 2 and not last:
                        turn_x(b + 1, 0, 1)
                    if c == 1 and t == TILES - 1 and not last:
                        turn_x(b + 1, 0, 3)
                    attend(b, t, c)
                    if c == 1 and t == TILES - 1 and not last:
                        project_g(b + 1, 0)
                    if c == 2 and t == TILES - 1 and not last:
                        score(b + 1, 0, 0)
                if more and k == 2:
                    project_v(b, GROUP * (g + 1))
                    project_g(b, g + 1)
                    for j in range(1, GROUP):
                        project_v(b, GROUP * (g + 1) + j)

            def batch(b, last):
                for t in range(PEELED, TILES):
                    tile(b, t, last)
                if not last:
                    project_v(b + 1, 0)
                    for t in range(PEELED):
                        tile(b + 1, t)

            pe.wait_ge(consts_ready, 3)
            turn_x(0, 0, 0)
            fold_weights(0, range(1))
            turn_x(0, 0, 1)
            fold_weights(0, range(1, DC))
            turn_x(0, 0, 2)
            fold_weights(1, range(1))
            turn_x(0, 0, 3)
            fold_weights(1, range(1, DC))
            project_g(0, 0, first=True)
            score(0, 0, 0)
            project_v(0, 0)
            for t in range(PEELED):
                tile(0, t, before=False)
            with pe.Fori(0, B - 1) as b:
                batch(b, False)
            batch(B - 1, True)

            def turn_x1(slot, c):
                for t in range(GROUP):
                    last = pe.transpose(psum[:, c, t * P:(t + 1) * P], x1_in[:, slot, t, c * P:(c + 1) * P], ident[:])
                last.then_inc(x1_turned, 1)

            def gate(i, n, before=False):
                if n == 0:
                    pe.wait_ge(gates_ready, 2 * i + 2)
                pe.wait_ge(h2_ready, 1 + i * 4 + (0 if before else n + 1))
                pe.matmul(psum[:, ACC, :], gates_s[:, n, :], h2_hi[:, n % 2, :], start=False, stop=False, skip_group_check=True)
                pe.matmul(psum[:, ACC, :], gates_s[:, n, :], h2_lo[:, n % 2, :], start=False, stop=False, skip_group_check=True).then_inc(gated, 1)

            def group(i, last_group, parity):
                pe.wait_ge(logits_copied, 1 + i)
                for c in range(DC):
                    pe.wait_ge(x1t_ready, i * DC + c + 1)
                    pe.matmul(psum[:, LOGIT, :], wr_s[:, c, :], x1t_hi[:, c, :], start=(c == 0), stop=False)
                    last = pe.matmul(psum[:, LOGIT, :], wr_s[:, c, :], x1t_lo[:, c, :], start=False, stop=(c == DC - 1))
                last.then_inc(logits_product, 1)
                for n in range(DC):
                    if n < 2:
                        pe.wait_ge(h2_hi_ready, 1 + i * 4 - 1 + n)
                    cols = slice(n * P, (n + 1) * P)
                    for c in range(DC):
                        last = split_product(pe, n, w1_hi[:, c, cols], w1_lo[:, c, cols], x1t_hi[:, c, :], x1t_lo[:, c, :], c == 0, c == DC - 1)
                    last.then_inc(h1_product, 1)
                    if n == 0:
                        gate(i, 3, before=True)
                        pe.wait_ge(logits_copied, 1 + i + 1)
                        for t in range(GROUP):
                            last = pe.transpose(psum[:, LOGIT_T, t * P:(t + 1) * P], logits_t[:, t * P:(t + 1) * P], ident[:])
                        last.then_inc(logits_turned, 1)
                if not last_group:
                    pe.wait_ge(x1_loaded[1 - parity], loads(parity))
                    for c in range(2):
                        pe.wait_ge(h1_hi_ready, 1 + i * 4 + c + 1)
                        turn_x1(1 - parity, c)
                for n in range(GROUP):
                    if n == 0:
                        pe.wait_ge(h1_hi_ready, 1 + i * 4 + 3)
                    if n == 2 and not last_group:
                        pe.wait_ge(x1t_ready, (i + 1) * DC + 2)
                    at = slice(n * P, (n + 1) * P)
                    for c in range(DC):
                        if n == 0:
                            pe.wait_ge(h1_ready, i * 4 + c + 1)
                        if n >= 2 and c == 1:
                            gate(i, n - 2)
                        last = split_product(pe, h2_bank(n), h1_hi[:, c, at], h1_lo[:, c, at], w3_hi[:, c, :], w3_lo[:, c, :], c == 0, c == DC - 1)
                    last.then_inc(h2_product, 1)
                    if n == 2 and not last_group:
                        for c in (2, 3):
                            pe.wait_ge(h2_hi_ready, 1 + i * 4 + c - 1)
                            turn_x1(1 - parity, c)
                gate(i, 2)

            pe.wait_ge(x1_loaded[0], DMA)
            pe.wait_ge(probs_ready, 1 + B * CHUNKS)
            for c in range(DC):
                turn_x1(0, c)
            pe.wait_ge(zeros_ready, 4)
            pe.matmul(psum[:, ACC, :], gates_s[:, 0, :], h2_hi[:, 0, :], start=True, stop=False, skip_group_check=True)
            pe.wait_ge(fold_ready, 1)
            pe.wait_ge(wr_split, 1)
            pe.wait_ge(w13_split, 2 * DC)
            with pe.Fori(0, NG // 2 - 1) as h:
                for parity in range(2):
                    def loads(parity_):
                        return h * DMA + (1 + parity_) * DMA
                    group(2 * h + parity, False, parity)

            def loads(parity_):
                return (NG // 2) * DMA
            group(NG - 2, False, 0)
            group(NG - 1, True, 1)
            gate(NG - 1, 3)
            pe.drain().then_inc(acc_done, 1)

            pe.wait_ge(acc_copied, 1)
            pe.wait_ge(h2_hi_ready, 1 + NG * 4)
            for c in range(DC):
                pe.matmul(psum[:, c, 0:P], acc_sb[:, c * P:(c + 1) * P], fold_rows[:], start=True, stop=True).then_inc(acc_turned, 1)
            pe.wait_ge(w2_loaded, DMA)
            for c in range(DC):
                pe.wait_ge(acc_t_ready, c + 1)
                last = pe.matmul(psum[:, FINAL, :], acc_t[:, c, :], w2_sb[:, c, :], start=(c == 0), stop=(c == DC - 1))
            last.then_inc(rows_product, 1)


def kernel(L0_attn_x, L0_attn_qkv, L0_attn_o_proj, L0_attn_gamma, L0_attn_beta, L0_ffn_w1, L0_ffn_w3, L0_ffn_w2, L0_ffn_wr):
    import numpy as np
    import concourse.bacc as bacc
    from concourse.bass_utils import run_bass_kernel_spmd

    x = np.asarray(L0_attn_x)
    qkv = np.asarray(L0_attn_qkv)
    arrays = {
        "x": x.reshape(-1, D),
        "wq_t": qkv[:, 0:D].T,
        "wk_t": qkv[:, D:2 * D].T,
        "wv_t": qkv[:, 2 * D:3 * D].T,
        "wo": np.asarray(L0_attn_o_proj),
        "gamma": np.asarray(L0_attn_gamma).reshape(DC, P).T,
        "beta": np.asarray(L0_attn_beta).reshape(DC, P).T,
        "w1_t": np.asarray(L0_ffn_w1).T,
        "w3_t": np.asarray(L0_ffn_w3).T,
        "w2_t": np.asarray(L0_ffn_w2).T,
        "wr_t": np.asarray(L0_ffn_wr).T,
    }
    arrays = {f"in_{k}": np.ascontiguousarray(a) for k, a in arrays.items()}
    nc = bacc.Bacc("TRN2", target_bir_lowering=False, num_devices=1)
    args = [nc.dram_tensor(k, a.shape, mybir.dt.from_np(a.dtype), kind="ExternalInput").ap() for k, a in arrays.items()]
    out = nc.dram_tensor("out_dram", arrays["in_x"].shape, F32, kind="ExternalOutput").ap()
    attention_mlp(nc, *args, out)
    r = run_bass_kernel_spmd(nc, [arrays], core_ids=[0])
    return r.results[0]["out_dram"].reshape(x.shape)
```
